# Optimizing a Trainium2 kernel written in Bass

```python
import numpy as np
import jax
import jax.numpy as jnp

def _softmax(x, axis=-1):
    return jax.nn.softmax(x, axis=axis)

def _gelu(x):
    return jax.nn.gelu(x, approximate=True)

def _silu(x):
    return jax.nn.silu(x)

def _sigmoid(x):
    return jax.nn.sigmoid(x)

def _layernorm(x, axis=-1, eps=1e-05):
    m = jnp.mean(x, axis=axis, keepdims=True)
    v = jnp.var(x, axis=axis, keepdims=True)
    return (x - m) / jnp.sqrt(v + eps)

def _scatter_add(tgt, idx, src, axis=0):
    return tgt.at[idx].add(src)

def _segment_sum(src, seg, n):
    return jax.ops.segment_sum(src, seg, n)
kernel_name = 'mk_gps_d2_gnn_r8_1b6e70'

def setup_inputs(seed: int=0):
    np.random.seed(seed)
    _w = jnp.asarray

    def _rec_inputs():
        import jax
        import jax.numpy as jnp
        _gk = jax.random.key(seed)
        x = -8.776e-05 + 1 * jax.random.normal(jax.random.fold_in(_gk, 1), (2500, 256), jnp.float32)
        _s = jax.random.randint(jax.random.fold_in(_gk, 2), (20000,), 0, 2500, jnp.int32)
        _d = jax.random.randint(jax.random.fold_in(_gk, 3), (20000,), 0, 2500, jnp.int32)
        _loop = jnp.arange(2500, dtype=jnp.int32)
        src = jnp.concatenate([_s, _d, _loop])
        dst = jnp.concatenate([_d, _s, _loop])
        _o = jnp.argsort(dst, stable=True)
        src = src[_o]
        dst = dst[_o]
        edge_type_8 = jax.random.randint(jax.random.fold_in(_gk, 13), (42500,), 0, 8, jnp.int32)
        return (x, src, dst, edge_type_8)
    x, src, dst, edge_type_8 = _rec_inputs()

    def _L0_gnn_setup():
        import jax, jax.numpy as jnp
        import numpy as np
        N_NODES = 2500
        N_EDGES = 37500
        D = 256
        NUM_RELS = 8
        NUM_BASES = 4
        key = jax.random.key(seed)
        ks = jax.random.split(key, 8)
        x = jax.random.normal(ks[0], (N_NODES, D), dtype=jnp.float32)
        src = jax.random.randint(ks[1], (N_EDGES,), 0, N_NODES, dtype=jnp.int32)
        dst = jax.random.randint(ks[2], (N_EDGES,), 0, N_NODES, dtype=jnp.int32)
        etypes = jax.random.randint(ks[3], (N_EDGES,), 0, NUM_RELS, dtype=jnp.int32)
        scale = 1.0 / np.sqrt(D)
        basis = jax.random.normal(ks[4], (NUM_BASES, D, D), dtype=jnp.float32) * scale
        comp = jax.random.normal(ks[5], (NUM_RELS, NUM_BASES), dtype=jnp.float32)
        loop_weight = jax.random.normal(ks[6], (D, D), dtype=jnp.float32) * scale
        bias_param = jnp.zeros((D,), dtype=jnp.float32)
        return {'x': x, 'src': src, 'dst': dst, 'etypes': etypes, 'basis': basis, 'comp': comp, 'loop_weight': loop_weight, 'bias_param': bias_param}
    _L0_gnn_all = _L0_gnn_setup()
    _L0_gnn_in = {k: v for k, v in _L0_gnn_all.items() if k in ('basis', 'comp', 'loop_weight', 'bias_param')}
    del _L0_gnn_all

    def _L0_mix_setup():
        import jax, jax.numpy as jnp
        import numpy as np
        A, Bc, Cc = (0.5, 1.0, 1.0)
        H = 8
        EPS = 1e-12

        def _normalize(t):
            n = jnp.linalg.norm(t, axis=-1, keepdims=True)
            return t / jnp.maximum(n, EPS)
        key = jax.random.key(seed)
        ks = jax.random.split(key, 5)
        B, N, C = (8, 256, 256)
        D = C // H
        x = jax.random.normal(ks[0], (B, N, C), dtype=jnp.float32)
        Wqkv = jax.random.normal(ks[1], (3 * H * D, C), dtype=jnp.float32) * 0.02
        bqkv = jnp.zeros((3 * H * D,), dtype=jnp.float32)
        Wproj = jax.random.normal(ks[2], (C, H * D), dtype=jnp.float32) * 0.02
        bproj = jnp.zeros((C,), dtype=jnp.float32)
        temperature = jnp.ones((1, H, 1, 1), dtype=jnp.float32)
        return {'x': x, 'Wqkv': Wqkv, 'bqkv': bqkv, 'Wproj': Wproj, 'bproj': bproj, 'temperature': temperature}
    _L0_mix_all = _L0_mix_setup()
    _L0_mix_in = {k: v for k, v in _L0_mix_all.items() if k in ('Wqkv', 'bqkv', 'Wproj', 'bproj', 'temperature')}
    del _L0_mix_all

    def _L0_ffn_setup():
        import jax, jax.numpy as jnp
        import numpy as np
        B, T, D, H, E = (16, 512, 256, 512, 8)
        key = jax.random.key(seed)
        ks = jax.random.split(key, 5)
        x = jax.random.normal(ks[0], (B, T, D), dtype=jnp.float32)
        gate_w = jax.random.normal(ks[1], (D, E), dtype=jnp.float32) * 0.02
        gate_b = jnp.zeros((E,), dtype=jnp.float32)
        W1 = jax.random.normal(ks[2], (E, D, H), dtype=jnp.float32) * 0.02
        b1 = jnp.zeros((E, H), dtype=jnp.float32)
        W2 = jax.random.normal(ks[3], (E, H, D), dtype=jnp.float32) * 0.02
        b2 = jnp.zeros((E, D), dtype=jnp.float32)
        return {'x': x, 'gate_w': gate_w, 'gate_b': gate_b, 'W1': W1, 'b1': b1, 'W2': W2, 'b2': b2}
    _L0_ffn_all = _L0_ffn_setup()
    _L0_ffn_in = {k: v for k, v in _L0_ffn_all.items() if k in ('gate_w', 'gate_b', 'W1', 'b1', 'W2', 'b2')}
    del _L0_ffn_all

    def _L1_gnn_setup():
        import jax, jax.numpy as jnp
        import numpy as np
        N_NODES = 6250
        N_EDGES = 50000
        IN_DIM = 256
        HID = 64
        HEADS = 8
        OUT_DIM = 256
        NEG_SLOPE = 0.2

        def _gat_forward(x, edge_index, W, a, Wo, bo):
            n = x.shape[0]
            src, tgt = (edge_index[0], edge_index[1])
            h = jnp.einsum('ni,hio->nho', x, W)
            a_src, a_tgt = (a[:, :HID], a[:, HID:])
            s_src = jnp.einsum('nho,ho->nh', h, a_src)
            s_tgt = jnp.einsum('nho,ho->nh', h, a_tgt)
            e = s_src[src] + s_tgt[tgt]
            e = jnp.where(e >= 0, e, NEG_SLOPE * e)
            m = jax.ops.segment_max(e, tgt, num_segments=n)
            ex = jnp.exp(e - m[tgt])
            denom = jax.ops.segment_sum(ex, tgt, num_segments=n)
            alpha = ex / (denom[tgt] + 1e-16)
            msgs = h[src] * alpha[:, :, None]
            out = jax.ops.segment_sum(msgs, tgt, num_segments=n)
            out = out.reshape(n, HEADS * HID)
            out = out @ Wo + bo
            return jax.nn.elu(out)
        key = jax.random.key(seed)
        ks = jax.random.split(key, 6)
        x = jax.random.normal(ks[0], (N_NODES, IN_DIM), dtype=jnp.float32)
        edge_index = jax.random.randint(ks[1], (2, N_EDGES), 0, N_NODES, dtype=jnp.int64)
        W = jax.random.normal(ks[2], (HEADS, IN_DIM, HID), dtype=jnp.float32) * (1.0 / np.sqrt(IN_DIM))
        a = jax.random.normal(ks[3], (HEADS, 2 * HID), dtype=jnp.float32) * (1.0 / np.sqrt(2 * HID))
        Wo = jax.random.normal(ks[4], (HEADS * HID, OUT_DIM), dtype=jnp.float32) * (1.0 / np.sqrt(HEADS * HID))
        bo = jnp.zeros((OUT_DIM,), dtype=jnp.float32)
        return {'x': x, 'edge_index': edge_index, 'W': W, 'a': a, 'Wo': Wo, 'bo': bo}
    _L1_gnn_all = _L1_gnn_setup()
    _L1_gnn_in = {k: v for k, v in _L1_gnn_all.items() if k in ('W', 'a', 'Wo', 'bo')}
    del _L1_gnn_all

    def _L1_mix_setup():
        import jax, jax.numpy as jnp
        import numpy as np
        NUM_HEADS = 8
        key = jax.random.key(seed)
        ks = jax.random.split(key, 5)
        B, N, C = (8, 2048, 256)
        x = jax.random.normal(ks[0], (B, N, C), dtype=jnp.float32)
        Wq = jax.random.normal(ks[1], (C, C), dtype=jnp.float32) * 0.02
        Wkv = jax.random.normal(ks[2], (2 * C, C), dtype=jnp.float32) * 0.02
        Wproj = jax.random.normal(ks[3], (C, C), dtype=jnp.float32) * 0.02
        bproj = jnp.zeros((C,), dtype=jnp.float32)
        return {'x': x, 'Wq': Wq, 'Wkv': Wkv, 'Wproj': Wproj, 'bproj': bproj}
    _L1_mix_all = _L1_mix_setup()
    _L1_mix_in = {k: v for k, v in _L1_mix_all.items() if k in ('Wq', 'Wkv', 'Wproj', 'bproj')}
    del _L1_mix_all

    def _L1_ffn_setup():
        import jax, jax.numpy as jnp
        import numpy as np
        BN_EPS = 0.001

        def _bn(h, g, b, m, v):
            return g * (h - m) * jax.lax.rsqrt(v + BN_EPS) + b
        key = jax.random.key(seed)
        ks = jax.random.split(key, 8)
        B, F, Df = (256, 64, 256)
        E, H, D = (8, 256, 256)
        s1 = 1.0 / np.sqrt(Df)
        s2 = 1.0 / np.sqrt(H)
        return {'x': jax.random.normal(ks[0], (B, F, Df), jnp.float32), 'Wr': jax.random.normal(ks[1], (Df, E), jnp.float32) * s1, 'br': jnp.zeros((E,), jnp.float32), 'W1': jax.random.normal(ks[2], (E, Df, H), jnp.float32) * s1, 'b1': jnp.zeros((E, H), jnp.float32), 'g1': jnp.ones((E, H), jnp.float32), 'be1': jnp.zeros((E, H), jnp.float32), 'm1': jnp.zeros((E, H), jnp.float32), 'v1': jnp.ones((E, H), jnp.float32), 'W2': jax.random.normal(ks[3], (E, H, H), jnp.float32) * s2, 'b2': jnp.zeros((E, H), jnp.float32), 'g2': jnp.ones((E, H), jnp.float32), 'be2': jnp.zeros((E, H), jnp.float32), 'm2': jnp.zeros((E, H), jnp.float32), 'v2': jnp.ones((E, H), jnp.float32), 'Wo': jax.random.normal(ks[4], (E, H, D), jnp.float32) * s2, 'bo': jnp.zeros((E, D), jnp.float32)}
    _L1_ffn_all = _L1_ffn_setup()
    _L1_ffn_in = {k: v for k, v in _L1_ffn_all.items() if k in ('Wr', 'br', 'W1', 'b1', 'g1', 'be1', 'm1', 'v1', 'W2', 'b2', 'g2', 'be2', 'm2', 'v2', 'Wo', 'bo')}
    del _L1_ffn_all
    return {'x': x, 'src': src, 'dst': dst, 'edge_type_8': edge_type_8, 'L0_gnn_basis': _L0_gnn_in['basis'], 'L0_gnn_comp': _L0_gnn_in['comp'], 'L0_gnn_loop_weight': _L0_gnn_in['loop_weight'], 'L0_gnn_bias_param': _L0_gnn_in['bias_param'], 'L0_mix_Wqkv': _L0_mix_in['Wqkv'], 'L0_mix_bqkv': _L0_mix_in['bqkv'], 'L0_mix_Wproj': _L0_mix_in['Wproj'], 'L0_mix_bproj': _L0_mix_in['bproj'], 'L0_mix_temperature': _L0_mix_in['temperature'], 'L0_ffn_gate_w': _L0_ffn_in['gate_w'], 'L0_ffn_gate_b': _L0_ffn_in['gate_b'], 'L0_ffn_W1': _L0_ffn_in['W1'], 'L0_ffn_b1': _L0_ffn_in['b1'], 'L0_ffn_W2': _L0_ffn_in['W2'], 'L0_ffn_b2': _L0_ffn_in['b2'], 'L1_gnn_W': _L1_gnn_in['W'], 'L1_gnn_a': _L1_gnn_in['a'], 'L1_gnn_Wo': _L1_gnn_in['Wo'], 'L1_gnn_bo': _L1_gnn_in['bo'], 'L1_mix_Wq': _L1_mix_in['Wq'], 'L1_mix_Wkv': _L1_mix_in['Wkv'], 'L1_mix_Wproj': _L1_mix_in['Wproj'], 'L1_mix_bproj': _L1_mix_in['bproj'], 'L1_ffn_Wr': _L1_ffn_in['Wr'], 'L1_ffn_br': _L1_ffn_in['br'], 'L1_ffn_W1': _L1_ffn_in['W1'], 'L1_ffn_b1': _L1_ffn_in['b1'], 'L1_ffn_g1': _L1_ffn_in['g1'], 'L1_ffn_be1': _L1_ffn_in['be1'], 'L1_ffn_m1': _L1_ffn_in['m1'], 'L1_ffn_v1': _L1_ffn_in['v1'], 'L1_ffn_W2': _L1_ffn_in['W2'], 'L1_ffn_b2': _L1_ffn_in['b2'], 'L1_ffn_g2': _L1_ffn_in['g2'], 'L1_ffn_be2': _L1_ffn_in['be2'], 'L1_ffn_m2': _L1_ffn_in['m2'], 'L1_ffn_v2': _L1_ffn_in['v2'], 'L1_ffn_Wo': _L1_ffn_in['Wo'], 'L1_ffn_bo': _L1_ffn_in['bo']}

def reference(x, src, dst, edge_type_8, L0_gnn_basis, L0_gnn_comp, L0_gnn_loop_weight, L0_gnn_bias_param, L0_mix_Wqkv, L0_mix_bqkv, L0_mix_Wproj, L0_mix_bproj, L0_mix_temperature, L0_ffn_gate_w, L0_ffn_gate_b, L0_ffn_W1, L0_ffn_b1, L0_ffn_W2, L0_ffn_b2, L1_gnn_W, L1_gnn_a, L1_gnn_Wo, L1_gnn_bo, L1_mix_Wq, L1_mix_Wkv, L1_mix_Wproj, L1_mix_bproj, L1_ffn_Wr, L1_ffn_br, L1_ffn_W1, L1_ffn_b1, L1_ffn_g1, L1_ffn_be1, L1_ffn_m1, L1_ffn_v1, L1_ffn_W2, L1_ffn_b2, L1_ffn_g2, L1_ffn_be2, L1_ffn_m2, L1_ffn_v2, L1_ffn_Wo, L1_ffn_bo):
    import jax
    import jax.numpy as jnp

    def _L0_gnn_ref(x, src, dst, etypes, basis, comp, loop_weight, bias_param):
        import jax, jax.numpy as jnp
        import numpy as np
        N_NODES = 2500
        N_EDGES = 37500
        D = 256
        NUM_RELS = 8
        NUM_BASES = 4
        W = jnp.einsum('rb,bio->rio', comp, basis)
        H = jnp.einsum('ni,rio->nro', x, W)
        msg = H[src, etypes]
        agg = jax.ops.segment_sum(msg, dst, num_segments=N_NODES)
        out = agg + x @ loop_weight + bias_param
        return out

    def _L0_mix_ref(x, Wqkv, bqkv, Wproj, bproj, temperature):
        import jax, jax.numpy as jnp
        import numpy as np
        A, Bc, Cc = (0.5, 1.0, 1.0)
        H = 8
        EPS = 1e-12

        def _normalize(t):
            n = jnp.linalg.norm(t, axis=-1, keepdims=True)
            return t / jnp.maximum(n, EPS)
        B, N, C = x.shape
        D = C // H
        scale = float(D) ** 0.25
        qkv = (x @ Wqkv.T + bqkv).reshape(B, N, 3, H, D)
        qkv = jnp.transpose(qkv, (2, 0, 3, 1, 4))
        q, k, v = (qkv[0], qkv[1], qkv[2])
        q = q * scale
        v1 = jnp.concatenate([jnp.ones((B, H, N, 1), dtype=v.dtype), v], axis=-1)
        qn = _normalize(q) * (scale * temperature)
        kn = _normalize(k) * scale
        vN = v1 / N
        kv_mod = jnp.einsum('bhni,bhnj,bhne->bhije', kn, kn, vN)
        kv = jnp.einsum('bhnd,bhne->bhde', kn, vN)
        vsum = jnp.sum(vN, axis=-2)[:, :, None, :]
        y = A * jnp.einsum('bhni,bhnj,bhije->bhne', qn, qn, kv_mod) + scale ** 2 * Bc * jnp.einsum('bhnd,bhde->bhne', qn, kv) + scale ** 4 * Cc * vsum
        y_norm, y = (y[..., :1], y[..., 1:])
        y = y / y_norm
        out = jnp.transpose(y, (0, 2, 1, 3)).reshape(B, N, H * D)
        return out @ Wproj.T + bproj

    def _L0_ffn_ref(x, gate_w, gate_b, W1, b1, W2, b2):
        import jax, jax.numpy as jnp
        import numpy as np
        B, T, D, H, E = (16, 512, 256, 512, 8)
        Bb, Tt, Dd = x.shape
        Ee = gate_w.shape[1]
        xf = x.reshape(-1, Dd)
        N = xf.shape[0]
        logits = xf @ gate_w + gate_b
        probs = jax.nn.softmax(logits, axis=-1)
        top2_vals, top2_idx = jax.lax.top_k(probs, 2)
        cw = jnp.zeros((N, Ee), dtype=xf.dtype).at[jnp.arange(N)[:, None], top2_idx].add(top2_vals)

        def step(acc, params):
            w1, bb1, w2, bb2, we = params
            h = jax.nn.gelu(xf @ w1 + bb1, approximate=False)
            y = h @ w2 + bb2
            return (acc + we[:, None] * y, None)
        out, _ = jax.lax.scan(step, jnp.zeros_like(xf), (W1, b1, W2, b2, cw.T))
        return out.reshape(Bb, Tt, Dd)

    def _L1_gnn_ref(x, edge_index, W, a, Wo, bo):
        import jax, jax.numpy as jnp
        import numpy as np
        N_NODES = 6250
        N_EDGES = 50000
        IN_DIM = 256
        HID = 64
        HEADS = 8
        OUT_DIM = 256
        NEG_SLOPE = 0.2

        def _gat_forward(x, edge_index, W, a, Wo, bo):
            n = x.shape[0]
            src, tgt = (edge_index[0], edge_index[1])
            h = jnp.einsum('ni,hio->nho', x, W)
            a_src, a_tgt = (a[:, :HID], a[:, HID:])
            s_src = jnp.einsum('nho,ho->nh', h, a_src)
            s_tgt = jnp.einsum('nho,ho->nh', h, a_tgt)
            e = s_src[src] + s_tgt[tgt]
            e = jnp.where(e >= 0, e, NEG_SLOPE * e)
            m = jax.ops.segment_max(e, tgt, num_segments=n)
            ex = jnp.exp(e - m[tgt])
            denom = jax.ops.segment_sum(ex, tgt, num_segments=n)
            alpha = ex / (denom[tgt] + 1e-16)
            msgs = h[src] * alpha[:, :, None]
            out = jax.ops.segment_sum(msgs, tgt, num_segments=n)
            out = out.reshape(n, HEADS * HID)
            out = out @ Wo + bo
            return jax.nn.elu(out)
        return _gat_forward(x, edge_index, W, a, Wo, bo)

    def _L1_mix_ref(x, Wq, Wkv, Wproj, bproj):
        import jax, jax.numpy as jnp
        import numpy as np
        NUM_HEADS = 8
        B, N, C = x.shape
        h = NUM_HEADS
        d = C // h
        q = jnp.einsum('bnc,oc->bno', x, Wq).reshape(B, N, h, d).transpose(0, 2, 1, 3)
        kv = jnp.einsum('bnc,oc->bno', x, Wkv).reshape(B, N, 2, h, d)
        k = kv[:, :, 0].transpose(0, 2, 1, 3)
        v = kv[:, :, 1].transpose(0, 2, 1, 3)
        q = jax.nn.elu(q) + 1.0
        k = jax.nn.elu(k) + 1.0
        k_sum = k.sum(axis=2)
        D_inv = 1.0 / jnp.maximum(jnp.einsum('bhnd,bhd->bhn', q, k_sum), 1e-06)
        context = jnp.einsum('bhnd,bhne->bhde', k, v)
        attn = jnp.einsum('bhnd,bhde->bhne', q, context) * D_inv[..., None]
        out = attn.transpose(0, 2, 1, 3).reshape(B, N, C)
        out = jnp.einsum('bnc,oc->bno', out, Wproj) + bproj
        return out

    def _L1_ffn_ref(x, Wr, br, W1, b1, g1, be1, m1, v1, W2, b2, g2, be2, m2, v2, Wo, bo):
        import jax, jax.numpy as jnp
        import numpy as np
        BN_EPS = 0.001

        def _bn(h, g, b, m, v):
            return g * (h - m) * jax.lax.rsqrt(v + BN_EPS) + b
        feat = jnp.mean(x, axis=0)
        w = jax.nn.softmax(feat @ Wr + br, axis=-1)
        h = jnp.einsum('bfd,edh->bfeh', x, W1) + b1
        h = jax.nn.relu(_bn(h, g1, be1, m1, v1))
        h = jnp.einsum('bfeh,ehk->bfek', h, W2) + b2
        h = jax.nn.relu(_bn(h, g2, be2, m2, v2))
        y = jnp.einsum('bfeh,ehd->bfed', h, Wo) + bo
        return jnp.einsum('bfed,fe->bfd', y, w)
    edge_index = jnp.stack([src, dst])
    xn = _layernorm(x, axis=-1)
    x = x + _L0_gnn_ref(xn, src, dst, edge_type_8, L0_gnn_basis, L0_gnn_comp, L0_gnn_loop_weight, L0_gnn_bias_param) + _L0_mix_ref(xn[None], L0_mix_Wqkv, L0_mix_bqkv, L0_mix_Wproj, L0_mix_bproj, L0_mix_temperature)[0]
    x = x + _L0_ffn_ref(_layernorm(x, axis=-1)[None], L0_ffn_gate_w, L0_ffn_gate_b, L0_ffn_W1, L0_ffn_b1, L0_ffn_W2, L0_ffn_b2)[0]
    xn = _layernorm(x, axis=-1)
    x = x + _L1_gnn_ref(xn, edge_index, L1_gnn_W, L1_gnn_a, L1_gnn_Wo, L1_gnn_bo) + _L1_mix_ref(xn[None], L1_mix_Wq, L1_mix_Wkv, L1_mix_Wproj, L1_mix_bproj)[0]
    x = x + _L1_ffn_ref(_layernorm(x, axis=-1)[None], L1_ffn_Wr, L1_ffn_br, L1_ffn_W1, L1_ffn_b1, L1_ffn_g1, L1_ffn_be1, L1_ffn_m1, L1_ffn_v1, L1_ffn_W2, L1_ffn_b2, L1_ffn_g2, L1_ffn_be2, L1_ffn_m2, L1_ffn_v2, L1_ffn_Wo, L1_ffn_bo)[0]
    return x

_drawn_inputs = setup_inputs


def setup_inputs(seed=0):
    import zlib

    import numpy as np

    out = dict(_drawn_inputs(seed))
    spreads = {'L0_gnn_bias_param': (0.0, 0.729),
     'L0_mix_bqkv': (0.0, 0.8),
     'L0_mix_bproj': (0.0, 0.671),
     'L0_mix_temperature': (1.0, 0.6),
     'L0_ffn_gate_b': (0.0, 0.8),
     'L0_ffn_b1': (0.0, 0.8),
     'L0_ffn_b2': (0.0, 0.8),
     'L1_gnn_bo': (0.0, 0.8),
     'L1_mix_bproj': (0.0, 0.712),
     'L1_ffn_br': (0.0, 0.8),
     'L1_ffn_b1': (0.0, 0.8),
     'L1_ffn_g1': (1.0, 0.6),
     'L1_ffn_be1': (0.0, 2.0),
     'L1_ffn_m1': (0.0, 0.8),
     'L1_ffn_v1': (1.0, 0.6),
     'L1_ffn_b2': (0.0, 0.8),
     'L1_ffn_g2': (1.0, 0.6),
     'L1_ffn_be2': (0.0, 2.0),
     'L1_ffn_m2': (0.0, 0.8),
     'L1_ffn_v2': (1.0, 0.6),
     'L1_ffn_bo': (0.0, 0.8)}
    factors = {'L0_mix_Wqkv': 8.0,
     'L0_mix_Wproj': 8.0,
     'L0_ffn_gate_w': 8.0,
     'L0_ffn_W1': 8.0,
     'L0_ffn_W2': 8.0,
     'L1_gnn_a': 3.922,
     'L1_mix_Wq': 50.825,
     'L1_mix_Wkv': 8.0,
     'L1_mix_Wproj': 8.0}
    for name, (base, spread) in spreads.items():
        noise = np.random.default_rng([zlib.crc32(name.encode()), seed]).standard_normal(out[name].shape)
        drawn = base * np.exp(spread * noise) if base else spread * noise
        out[name] = jnp.asarray(drawn.astype(out[name].dtype))
    for name, factor in factors.items():
        out[name] = (out[name] * factor).astype(out[name].dtype)
    return out
```

```python
from contextlib import ExitStack, contextmanager

import concourse.bass as bass
from concourse import mybir

F32 = mybir.dt.float32
F16 = mybir.dt.float16
I32 = mybir.dt.int32
ALU = mybir.AluOpType
ACT = mybir.ActivationFunctionType
AX = mybir.AxisListType.X
ds = bass.ds

P = 128
N = 2500
T = -(-N // P)
NP = T * P
LAST = N - (T - 1) * P
D = 256
K = D // P
E = 42500
EP, EC = 125, 340
assert EP * EC == E
R = 8
NB = 4
H = 8
DH = D // H
SUP = 4
NSUP = (E + T * (SUP * P - 1)) // (SUP * P)
NSLOT = NSUP * SUP
LN_EPS = 1e-5
QUAD = (DH // 2 + 1) * DH
FEAT = QUAD + DH + 1
FS = [(s * P, min(P, FEAT - s * P)) for s in range(-(-FEAT // P))]
GT = 4
NG = T // GT


class Link:

    def __init__(self, eng, sem):
        self.eng, self.sem, self.base, self.k = eng, sem, 0, 0

    def inc(self, ins):
        ins.then_inc(self.sem, 1)
        self.k += 1

    def __call__(self, ins):
        self.inc(ins)
        self.eng.wait_ge(self.sem, self.base + self.k)

    @contextmanager
    def loop(self, n, per):
        start = self.base + self.k
        with self.eng.Fori(0, n) as i:
            self.base, self.k = start + i * per, 0
            yield i
            assert self.k == per, f"{self.k} steps in a round, not {per}"
        self.base, self.k = start + n * per, 0


def hold(eng, sem, value, held):
    eng.wait_ge(sem, value)
    eng.sem_inc(held, 1)


class Store:
    pass


def tensors(nc, ctx):
    def sb(name, shape, dt=F32):
        return ctx.enter_context(nc.sbuf_tensor(name, shape, dt))

    def ps(name, shape, dt=F32):
        return ctx.enter_context(nc.psum_tensor(name, shape, dt))

    sems = []

    def sem(name):
        sems.append(nc.alloc_semaphore(name))
        return sems[-1]

    @ctx.callback
    def _():
        nc.clear_and_free_semaphores(sems)
        nc.all_engine_barrier()

    return sb, ps, sem


def layernorm_stats(dve, link, st, stats, mean, var):
    with link.loop(T, 1) as t:
        link.inc(dve.bn_stats(stats[:, ds(t * 6, 6)], st.x[:, ds(t * D, D)]))
    dve.wait_ge(link.sem, link.base + link.k)
    s = stats[:, :].rearrange("p (t c) -> p t c", c=6)
    link.inc(dve.tensor_tensor(mean[:, :], s[:, :, 1], s[:, :, 4], ALU.add))
    link.inc(dve.tensor_tensor(s[:, :, 0], s[:, :, 1], s[:, :, 4], ALU.subtract))
    link(dve.tensor_tensor(var[:, :], s[:, :, 2], s[:, :, 5], ALU.add))
    link.inc(dve.tensor_scalar(mean[:, :], mean[:, :], 0.5, None, ALU.mult))
    link.inc(dve.tensor_scalar(var[:, :], var[:, :], 1.0 / D, LN_EPS, ALU.mult, ALU.add))
    link(dve.scalar_tensor_tensor(out=s[:, :, 3], in0=s[:, :, 0], scalar=0.25, in1=s[:, :, 0], op0=ALU.mult, op1=ALU.mult))
    link(dve.tensor_tensor(var[:, :], var[:, :], s[:, :, 3], ALU.add))


def slot_edges(nc, io, st):
    with ExitStack() as ctx:
        sb, ps, sem = tensors(nc, ctx)
        dst_i = sb("dst_i", [EP, EC], I32)
        src_i = sb("src_i", [EP, EC], I32)
        et_i = sb("et_i", [EP, EC], I32)
        e_a = sb("e_a", [EP, EC])
        e_b = sb("e_b", [EP, EC])
        e_i = sb("e_i", [EP, EC], I32)
        e_tile = sb("e_tile", [EP, EC])
        hot = sb("hot", [EP, T, EC], F16)
        keep = sb("keep", [EP, T, EC], F16)
        col0 = sb("col0", [EP, T])
        first = sb("first", [EP, T])
        scan = sb("scan", [EP, T, EC])
        iota_t = sb("iota_t", [P, T])
        upper = sb("upper", [P, P])
        ones = sb("ones", [P, P])
        tcount = sb("tcount", [EP, T])
        need = sb("need", [P, T])
        need_i = sb("need_i", [P, T], I32)
        cum = sb("cum", [P, T])
        ones_t = sb("ones_t", [P, T])
        base = sb("base", [P, T])
        cmp_s = sb("cmp_s", [1, NSUP, T])
        tos = sb("tos", [1, NSUP])
        sup_i = sb("sup_i", [1, NSUP])
        p_t = ps("p_c", [P, 2, D])
        x_cleared = sem("x_cleared")
        x_in = sem("x_in")
        edges_in = sem("edges_in")
        made = sem("made")
        consts = sem("consts")
        dv = sem("dv")
        counted = sem("counted")
        prefixed = sem("prefixed")
        block = ctx.enter_context(nc.Block())
        NCONST = 15

        @block.sync
        def _(sp):
            sp.dma_start(st.x[:, 0:(T - 1) * D].rearrange("p (t d) -> p t d", d=D),
                         io["x"][0:(T - 1) * P, :].rearrange("(t p) d -> p t d", p=P)).then_inc(x_in, 16)
            sp.wait_ge(x_cleared, 1)
            sp.dma_start(st.x[0:LAST, (T - 1) * D:T * D], io["x"][(T - 1) * P:N, :]).then_inc(x_in, 16)
            sp.wait_ge(x_in, 32)

        @block.gpsimd
        def _(pool):
            pool.dma_start(dst_i[:, :], io["dst"].rearrange("(p c) -> p c", p=EP)).then_inc(edges_in, 16)
            pool.dma_start(src_i[:, :], io["src"].rearrange("(p c) -> p c", p=EP)).then_inc(edges_in, 16)
            pool.dma_start(et_i[:, :], io["edge_type_8"].rearrange("(p c) -> p c", p=EP)).then_inc(edges_in, 16)
            pool.memset(st.x[:, (T - 1) * D:T * D], 0.0).then_inc(x_cleared, 1)
            pool.iota(iota_t[:, :], pattern=[[1, T]], base=0, channel_multiplier=0, allow_small_or_imprecise_dtypes=True).then_inc(consts, 1)
            pool.iota(st.iota_s[:, :], pattern=[[1, NSLOT]], base=0, channel_multiplier=0, allow_small_or_imprecise_dtypes=True).then_inc(consts, 1)
            pool.iota(st.iota_h[:, :], pattern=[[1, P]], base=0, channel_multiplier=0, allow_small_or_imprecise_dtypes=True).then_inc(consts, 1)
            pool.iota(st.iota[:, :], pattern=[[1, P]], base=0, channel_multiplier=0, allow_small_or_imprecise_dtypes=True).then_inc(consts, 1)
            pool.iota(sup_i[:, :], pattern=[[1, NSUP]], base=0, channel_multiplier=0, allow_small_or_imprecise_dtypes=True).then_inc(consts, 1)
            pool.memset(st.dloc[:, NSLOT:], -1.0).then_inc(consts, 1)
            pool.memset(st.row_src[:, NSLOT:], 0).then_inc(consts, 1)
            pool.memset(st.tile_of[:, NSUP:], 0).then_inc(consts, 1)
            pool.memset(ones[:, :], 1.0).then_inc(consts, 1)
            pool.memset(ones_t[:, :], 1.0).then_inc(consts, 1)
            pool.memset(st.v1[:, :], 1.0).then_inc(consts, 1)
            pool.memset(st.ident[:, :], 0.0).then_inc(made, 1)
            pool.memset(upper[:, :], 1.0).then_inc(made, 1)
            pool.memset(st.rowmask[:, :], 1.0).then_inc(made, 1)
            pool.memset(keep[:, :, :], 1.0).then_inc(made, 1)
            pool.wait_ge(made, 4)
            pool.affine_select(out=st.ident[:, :], in_=st.ident[:, :], compare_op=ALU.not_equal, fill=1.0,
                               base=0, pattern=[[-1, P]], channel_multiplier=1).then_inc(consts, 1)
            pool.affine_select(out=upper[:, :], in_=upper[:, :], compare_op=ALU.is_gt, fill=0.0,
                               base=0, pattern=[[1, P]], channel_multiplier=-1).then_inc(consts, 1)
            pool.affine_select(out=st.rowmask[:, :], in_=st.rowmask[:, :], compare_op=ALU.is_gt, fill=0.0,
                               base=LAST, pattern=[[0, 1]], channel_multiplier=-1).then_inc(consts, 1)
            pool.memset(keep[:, :, 0:1], 0.0).then_inc(consts, 1)

        @block.vector
        def _(dve):
            link = Link(dve, dv)
            dve.wait_ge(consts, NCONST)
            dve.wait_ge(edges_in, 48)
            link.inc(dve.tensor_scalar(e_i[:, :], dst_i[:, :], 7, None, ALU.logical_shift_right))
            link(dve.tensor_scalar(dst_i[:, :], dst_i[:, :], P - 1, None, ALU.bitwise_and))
            link.inc(dve.tensor_copy(e_tile[:, :], e_i[:, :]))
            link(dve.tensor_scalar(e_a[:, :], src_i[:, :], float(R * P), 1.0, ALU.mult, ALU.add))
            link(dve.scalar_tensor_tensor(out=e_b[:, :], in0=et_i[:, :], scalar=float(P), in1=e_a[:, :], op0=ALU.mult, op1=ALU.add))
            link(dve.tensor_tensor(e_i[:, :], e_b[:, :], dst_i[:, :], ALU.add))
            link.inc(dve.tensor_scalar(src_i[:, :], e_i[:, :], 11, None, ALU.logical_shift_right))
            link(dve.tensor_scalar(et_i[:, :], e_i[:, :], 2047, None, ALU.bitwise_and))
            link.inc(dve.tensor_copy(st.rec_hi[:, :], src_i[:, :]))
            link.inc(dve.tensor_copy(st.rec_lo[:, :], et_i[:, :]))
            link(dve.tensor_tensor(hot[:, :, :], e_tile[:, :].unsqueeze(1).broadcast_to([EP, T, EC]),
                                   iota_t[0:EP, :].unsqueeze(2).broadcast_to([EP, T, EC]), ALU.is_equal))
            link(dve.tensor_reduce(tcount[:, :], hot[:, :, :], AX, ALU.add))
            dve.sem_inc(counted, 1)
            dve.wait_ge(prefixed, 1)
            link(dve.tensor_scalar(need_i[:, :], p_t[:, 0, 0:T], float(SUP * P - 1), None, ALU.add))
            link(dve.tensor_scalar(need_i[:, :], need_i[:, :], 9, None, ALU.logical_shift_right))
            link(dve.tensor_copy(need[:, :], need_i[:, :]))
            link(dve.tensor_tensor_scan(cum[:, :], ones_t[:, :], need[:, :], 0.0, ALU.mult, ALU.add))
            link(dve.tensor_tensor(cum[:, :], cum[:, :], need[:, :], ALU.subtract))
            link(dve.tensor_scalar(base[:, :], cum[:, :], float(SUP * P), -1.0, ALU.mult, ALU.add))
            link(dve.tensor_tensor(base[0:EP, :], base[0:EP, :], p_t[0:EP, 1, 0:T], ALU.add))
            link(dve.tensor_tensor(cmp_s[:, :, :], cum[0:1, :].unsqueeze(1).broadcast_to([1, NSUP, T]),
                                   sup_i[:, :].unsqueeze(2).broadcast_to([1, NSUP, T]), ALU.is_le))
            link(dve.tensor_reduce(tos[:, :], cmp_s[:, :, :], AX, ALU.add))
            link(dve.tensor_scalar(st.tile_of[:, 0:NSUP], tos[:, :], -1.0, None, ALU.add))
            link(dve.tensor_copy(col0[:, :], hot[:, :, 0]))
            link(dve.tensor_tensor(first[:, :], col0[:, :], base[0:EP, :], ALU.add))
            link(dve.tensor_copy(scan[:, :, :], hot[:, :, :]))
            link(dve.tensor_copy(scan[:, :, 0], first[:, :]))
            flat = "p t c -> p (t c)"
            link(dve.tensor_tensor_scan(scan[:, :, :].rearrange(flat), keep[:, :, :].rearrange(flat),
                                        scan[:, :, :].rearrange(flat), 0.0, ALU.mult, ALU.add))
            link(dve.tensor_tensor(scan[:, :, :], scan[:, :, :], hot[:, :, :], ALU.mult))
            link(dve.tensor_reduce(e_a[:, :], scan[:, :, :].rearrange("p t c -> p c t"), AX, ALU.add))
            link(dve.tensor_copy(dst_i[:, :], e_a[:, :]))
            link.inc(dve.tensor_scalar(src_i[:, :], dst_i[:, :], 7, None, ALU.logical_shift_right))
            link(dve.tensor_scalar(et_i[:, :], dst_i[:, :], P - 1, None, ALU.bitwise_and))
            link.inc(dve.tensor_copy(st.slot_hi[:, :], src_i[:, :]))
            link(dve.tensor_copy(st.slot_lo[:, :], et_i[:, :]))

        @block.tensor
        def _(pe):
            pe.wait_ge(consts, NCONST)
            pe.wait_ge(counted, 1)
            pe.matmul(p_t[:, 0, 0:T], ones[0:EP, :], tcount[:, :], start=True, stop=True)
            pe.matmul(p_t[0:EP, 1, 0:T], upper[0:EP, 0:EP], tcount[:, :], start=True, stop=True).then_inc(prefixed, 1)


def front0(nc, io, st):
    with ExitStack() as ctx:
        sb, ps, sem = tensors(nc, ctx)
        CB = EC // T
        lo_hi = sb("lo_hi", [EP, 2, CB, 2, P], F16)
        hi_hot = sb("hi_hot", [EP, 2, CB, NSLOT], F16)
        zero = sb("zero", [P, P], F16)
        v_f = sb("v_f", [P, NSLOT])
        v_i = sb("v_i", [P, NSLOT], I32)
        v_j = sb("v_j", [P, NSLOT], I32)
        ok_f = sb("ok_f", [P, NSLOT])
        stats = sb("stats", [P, T * 6])
        mean = sb("mean", [P, T])
        rstd = sb("rstd", [P, T])
        sd = sb("sd", [P, T])
        xn = sb("xn", [P, 2, D])
        xT = sb("xT", [P, 2, D])
        basis = sb("basis", [P, NB, K, D])
        comp = sb("comp", [P, R * NB])
        w_rel = sb("w_rel", [P, K, R * D])
        w_lv = sb("w_lv", [P, K, 2 * D])
        w_qk = sb("w_qk", [P, K, 2 * D])
        b_qk = sb("b_qk", [P, 2 * D])
        b_v = sb("b_v", [P, D])
        h_out = sb("h_out", [P, 2, R * D])
        sq = sb("sq", [P, 2 * D])
        cvec = sb("cvec", [P, 2 * H])
        gvec = sb("gvec", [P, 2 * H])
        temp = sb("temp", [P, H])
        p_t = ps("p_t", [P, 2, 512])
        p_h = ps("p_h", [P, 2, 512])
        p_lv = ps("p_lv", [P, 512])
        p_qk = ps("p_qk", [P, 512])
        p_rec = ps("p_rec", [P, 2, 512])

        w_in = sem("w_in")
        dv = sem("dv1")
        var_ready = sem("var_ready")
        sd_ready = sem("sd_ready")
        w_ready = sem("w_ready")
        zeroed = sem("zeroed")
        ss_ready = sem("ss_ready")
        nrm_ready = sem("nrm_ready")
        xn_ready = sem("xn_ready")
        transposed = sem("transposed")
        xT_ready = sem("xT_ready")
        lv_ready = sem("lv_ready")
        lv_used = sem("lv_used")
        qk_ready = sem("qk_ready")
        qk_used = sem("qk_used")
        h_ready = sem("h_ready")
        h_copied = sem("h_copied")
        h_stored = sem("h_stored")
        h_free = sem("h_free")
        hot_ready = sem("hot_ready")
        hot_used = sem("hot_used")
        rec_ready = sem("rec_ready")

        block = ctx.enter_context(nc.Block())

        @block.sync
        def _(sp):
            for b in range(NB):
                sp.dma_start(basis[:, b], io["L0_gnn_basis"][b].rearrange("(k p) o -> p k o", p=P)).then_inc(w_in, 16)
            sp.dma_start(comp[:, :], io["L0_gnn_comp"].rearrange("r b -> (r b)").partition_broadcast(P)).then_inc(w_in, 16)
            sp.dma_start(w_lv[:, :, 0:D], io["L0_gnn_loop_weight"].rearrange("(k p) o -> p k o", p=P)).then_inc(w_in, 16)
            sp.dma_start(w_lv[:, :, D:], io["wqkv0"][:, 2 * D:].rearrange("(k p) o -> p k o", p=P)).then_inc(w_in, 16)
            sp.dma_start(w_qk[:, :, :], io["wqkv0"][:, 0:2 * D].rearrange("(k p) o -> p k o", p=P)).then_inc(w_in, 16)
            sp.dma_start(b_qk[:, :], io["L0_mix_bqkv"][0:2 * D].partition_broadcast(P)).then_inc(w_in, 16)
            sp.dma_start(b_v[:, :], io["L0_mix_bqkv"][2 * D:].partition_broadcast(P)).then_inc(w_in, 16)
            sp.dma_start(temp[:, :], io["temp0"].partition_broadcast(P)).then_inc(w_in, 16)
            sp.sem_inc(h_free, 2)
            with sp.Fori(0, T // 2) as i:
                for u in range(2):
                    sp.wait_ge(h_copied, (2 * i + u + 1) * 4 + 2)
                    sp.dma_start(st.h_table[ds((2 * i + u) * P, P), :], h_out[:, u]).then_inc(h_stored, 16)
                    sp.wait_ge(h_stored, (2 * i + u + 1) * 16)
                    sp.sem_inc(h_free, 1)

        NW = NB + 7

        @block.vector
        def _(dve):
            link = Link(dve, dv)
            dve.memset(zero[:, :], 0.0).then_inc(zeroed, 1)
            dve.sem_inc(hot_ready, 2)

            def hots(g, u):
                dve.wait_ge(hot_used, g + 1)
                for j in range(CB):
                    c = g * CB + j
                    lo = st.slot_lo[:, ds(c, 1)]
                    dve.tensor_scalar(lo_hi[:, u, j, 0], st.iota_h[0:EP, :], lo, st.rec_hi[:, ds(c, 1)], ALU.is_equal, ALU.mult)
                    dve.tensor_scalar(lo_hi[:, u, j, 1], st.iota_h[0:EP, :], lo, st.rec_lo[:, ds(c, 1)], ALU.is_equal, ALU.mult)
                    last = dve.tensor_scalar(hi_hot[:, u, j], st.iota_s[0:EP, :], st.slot_hi[:, ds(c, 1)], None, ALU.is_equal)
                last.then_inc(hot_ready, 1)

            layernorm_stats(dve, link, st, stats, mean, sd)
            dve.sem_inc(var_ready, 1)

            hots(0, 0)
            hots(1, 1)
            dve.wait_ge(w_in, 16 * NW)
            for r in range(R):
                out = w_rel[:, :, r * D:(r + 1) * D]
                for b in range(NB):
                    c = comp[:, r * NB + b:r * NB + b + 1]
                    if b == 0:
                        link(dve.tensor_scalar(out, basis[:, b], c, None, ALU.mult))
                    else:
                        link(dve.scalar_tensor_tensor(out=out, in0=basis[:, b], scalar=c, in1=out, op0=ALU.mult, op1=ALU.add))
            dve.sem_inc(w_ready, 1)
            dve.wait_ge(sd_ready, 1)
            link(dve.reciprocal(rstd[:, :], sd[:, :]))

            def norm(t, u):
                dve.wait_ge(transposed, t + 1)
                dve.tensor_scalar(xn[:, u], st.x[:, ds(t * D, D)], mean[:, ds(t, 1)], rstd[:, ds(t, 1)],
                                  ALU.subtract, ALU.mult).then_inc(xn_ready, 1)

            dve.sem_inc(lv_used, 1)
            dve.sem_inc(qk_used, 1)
            dve.sem_inc(xn_ready, 2)
            qk_t = st.qk.rearrange("p (g n) -> p g n", g=2 * H)
            v1_t = st.v1.rearrange("p (h n) -> p h n", h=H)

            def take(t, u):
                dve.wait_ge(lv_ready, t + 1)
                link.inc(dve.tensor_tensor(v1_t[:, :, ds(t * (DH + 1), DH)],
                                           p_lv[:, D:].rearrange("p (h e) -> p h e", h=H),
                                           b_v[:, :].rearrange("p (h e) -> p h e", h=H), ALU.add))
                dve.tensor_tensor(st.x[:, ds(t * D, D)], st.x[:, ds(t * D, D)], p_lv[:, 0:D], ALU.add).then_inc(lv_used, 1)
                dve.wait_ge(qk_ready, t + 1)
                part = qk_t[:, :, ds(t * DH, DH)]
                link(dve.tensor_tensor(part, p_qk[:, :].rearrange("p (g e) -> p g e", g=2 * H),
                                       b_qk[:, :].rearrange("p (g e) -> p g e", g=2 * H), ALU.add))
                dve.sem_inc(qk_used, 1)
                sq_t = sq[:, :].rearrange("p (g e) -> p g e", g=2 * H)
                link(dve.tensor_tensor(sq_t, part, part, ALU.mult))
                link(dve.tensor_reduce(st.nrm[:, :].rearrange("p (g t) -> p g t", g=2 * H)[:, :, ds(t, 1)], sq_t, AX, ALU.add))

            norm(0, 0)
            norm(1, 1)
            with link.loop(T // 2 - 1, 8) as i:
                for u in range(2):
                    norm(2 * i + 2 + u, u)
                    take(2 * i + u, u)
                    hots(2 * i + 2 + u, u)
            for u in range(2):
                take(T - 2 + u, u)
            tail = v1_t[:, :, (T - 1) * (DH + 1):T * (DH + 1)]
            link(dve.tensor_scalar(tail, tail, st.rowmask[:, 0:1], None, ALU.mult))
            dve.sem_inc(ss_ready, 1)
            scale = float(DH) ** 0.25
            link.inc(dve.memset(cvec[:, 0:H], scale))
            link.inc(dve.memset(cvec[:, H:], 1.0))
            link.inc(dve.memset(gvec[:, H:], scale))
            link(dve.tensor_scalar(gvec[:, 0:H], temp[:, :], scale * scale, None, ALU.mult))
            dve.wait_ge(nrm_ready, 1)
            nrm3 = st.nrm[:, :].rearrange("p (g t) -> p g t", g=2 * H)
            link(dve.tensor_tensor(nrm3, nrm3, cvec[:, :].unsqueeze(2).broadcast_to([P, 2 * H, T]), ALU.mult))
            link(dve.tensor_scalar(st.nrm[:, :], st.nrm[:, :], 1e-12, None, ALU.max))
            link(dve.reciprocal(st.nrm[:, :], st.nrm[:, :]))
            link(dve.tensor_tensor(nrm3, nrm3, gvec[:, :].unsqueeze(2).broadcast_to([P, 2 * H, T]), ALU.mult))

            dve.wait_ge(rec_ready, 1)
            link(dve.tensor_scalar(v_f[:, :], p_rec[:, 0, 0:NSLOT], 2048.0, -1.0, ALU.mult, ALU.add))
            link(dve.tensor_tensor(v_f[:, :], v_f[:, :], p_rec[:, 1, 0:NSLOT], ALU.add))
            link.inc(dve.tensor_scalar(ok_f[:, :], v_f[:, :], 0.0, None, ALU.is_ge))
            link(dve.tensor_scalar(v_i[:, :], v_f[:, :], 0.0, None, ALU.max))
            link.inc(dve.tensor_scalar(st.row_rel[:, 0:NSLOT], v_i[:, :], 7, None, ALU.logical_shift_right))
            link.inc(dve.tensor_scalar(st.row_src[:, 0:NSLOT], v_i[:, :], 10, None, ALU.logical_shift_right))
            link(dve.tensor_scalar(v_j[:, :], v_i[:, :], P - 1, None, ALU.bitwise_and))
            link(dve.tensor_copy(v_f[:, :], v_j[:, :]))
            link(dve.scalar_tensor_tensor(out=v_f[:, :], in0=v_f[:, :], scalar=1.0, in1=ok_f[:, :], op0=ALU.add, op1=ALU.mult))
            link(dve.tensor_scalar(st.dloc[:, 0:NSLOT], v_f[:, :], -1.0, None, ALU.add))

        @block.scalar
        def _(act):
            act.wait_ge(var_ready, 1)
            nc.scalar.activation(sd[:, :], sd[:, :], ACT.Sqrt).then_inc(sd_ready, 1)
            act.sem_inc(xT_ready, 2)
            act.sem_inc(h_copied, 2)
            with act.Fori(0, T // 2) as i:
                for u in range(2):
                    t = 2 * i + u
                    act.wait_ge(transposed, t + 3)
                    nc.scalar.copy(xT[:, u], p_t[:, u, 0:D]).then_inc(xT_ready, 1)
                for u in range(2):
                    t = 2 * i + u
                    act.wait_ge(h_free, t + 1)
                    for q in range(4):
                        act.wait_ge(h_ready, 4 * t + q + 1)
                        nc.scalar.copy(h_out[:, u, q * 512:(q + 1) * 512], p_h[:, q % 2]).then_inc(h_copied, 1)
            act.wait_ge(ss_ready, 1)
            nc.scalar.activation(st.nrm[:, :], st.nrm[:, :], ACT.Sqrt).then_inc(nrm_ready, 1)

        @block.tensor
        def _(pe):
            pe.sem_inc(transposed, 2)
            pe.sem_inc(hot_used, 2)
            pe.wait_ge(w_ready, 1)
            pe.wait_ge(zeroed, 1)
            for h in range(2):
                pe.matmul(p_rec[:, h, 0:NSLOT], zero[0:EP, :], st.iota_s[0:EP, :], start=True, stop=False, skip_group_check=True)

            with pe.Fori(0, T // 2) as i:
                for u in range(2):
                    t = 2 * i + u
                    pe.wait_ge(xn_ready, t + 3)
                    pe.wait_ge(xT_ready, t + 1)
                    for k in range(K):
                        last = pe.transpose(p_t[:, u, k * P:(k + 1) * P], xn[:, u, k * P:(k + 1) * P], st.ident[:, :])
                    last.then_inc(transposed, 1)
                for u in range(2):
                    t = 2 * i + u
                    pe.wait_ge(xT_ready, t + 3)
                    for out, w, free, ready in ((p_lv, w_lv, lv_used, lv_ready), (p_qk, w_qk, qk_used, qk_ready)):
                        pe.wait_ge(free, t + 1)
                        for k in range(K):
                            last = pe.matmul(out[:, :], xT[:, u, k * P:(k + 1) * P], w[:, k], start=k == 0, stop=k == K - 1)
                        last.then_inc(ready, 1)
                    for q in range(4):
                        pe.wait_ge(h_copied, 4 * t + q + 1)
                        for k in range(K):
                            last = pe.matmul(p_h[:, q % 2], xT[:, u, k * P:(k + 1) * P], w_rel[:, k, q * 512:(q + 1) * 512],
                                             start=k == 0, stop=k == K - 1)
                        last.then_inc(h_ready, 1)
                    pe.wait_ge(hot_ready, t + 3)
                    for j in range(CB):
                        for h in range(2):
                            last = pe.matmul(p_rec[:, h, 0:NSLOT], lo_hi[:, u, j, h], hi_hot[:, u, j],
                                             start=False, stop=False, skip_group_check=True)
                    last.then_inc(hot_used, 1)
            for h in range(2):
                last = pe.matmul(p_rec[:, h, 0:NSLOT], zero[0:EP, :], st.iota_s[0:EP, :], start=False, stop=True, skip_group_check=True)
            last.then_inc(rec_ready, 1)


def mix0_and_gather(nc, io, st):
    PER_HEAD = NSUP // H
    PER_HEAD -= PER_HEAD % 6
    TAIL = NSUP - H * PER_HEAD
    RING = 6
    AHEAD = 4
    with ExitStack() as ctx:
        sb, ps, sem = tensors(nc, ctx)
        kq = sb("kq", [P, 2, T, 48])
        feat = sb("feat", [P, 2, GT, FEAT])
        fT = sb("fT", [P, 2, len(FS), P])
        kvs = sb("kvs", [P, len(FS), DH + 1])
        w_f = sb("w_f", [P, len(FS)])
        r_y = sb("r_y", [P, GT])
        rows = sb("rows", [P, RING, SUP, D])
        idx = sb("idx", [P, RING, SUP], I32)
        oh = sb("oh", [P, RING, SUP, P])
        p_kv = ps("p_kv", [P, len(FS), DH + 1])
        p_ta = ps("p_ta", [P, 2, 4, P])
        p_tb = ps("p_tb", [P, 2, 512])
        p_y = ps("p_y", [P, GT, DH + 1])
        p_agg = ps("p_agg", [P, 2, 512])

        dv = sem("dv2")
        f_ready = sem("f_ready")
        f_used = sem("f_used")
        kvs_ready = sem("kvs_ready")
        t_ready = sem("t_ready")
        fT_ready = sem("fT_ready")
        y_ready = sem("y_ready")
        y_used = sem("y_used")
        oh_ready = sem("oh_ready")
        idx_ready = sem("idx_ready")
        held = sem("held")
        agg_done = sem("agg_done")
        agg_added = sem("agg_added")
        gathered = [sem(f"gathered{r}") for r in range(RING)]
        block = ctx.enter_context(nc.Block())

        share = [PER_HEAD * (g + 1) // (2 * NG) - PER_HEAD * g // (2 * NG) for g in range(2 * NG)]
        before = [sum(share[:g]) for g in range(2 * NG)]

        @block.gpsimd
        def _(pool):
            def gather(s, r):
                hold(pool, agg_done, s + 1, held)
                pool.tensor_copy(idx[:, r], st.row_rel[:, ds(s * SUP, SUP)]).then_inc(idx_ready, 1)
                hold(pool, idx_ready, s + 1, held)
                for j in range(SUP):
                    pool.indirect_dma_start(rows[:, r, j], None, st.h_rows,
                                            bass.IndirectOffsetOnAxis(ap=idx[:, r, j:j + 1], axis=0)
                                            ).then_inc(gathered[r], 16)

            with pool.Fori(0, H * PER_HEAD // RING) as i:
                for r in range(RING):
                    gather(i * RING + r, r)
            for s in range(H * PER_HEAD, NSUP):
                gather(s, s % RING)

        @block.vector
        def _(dve):
            link = Link(dve, dv)
            link.inc(dve.memset(feat[:, :, :, FEAT - 1:FEAT], 1.0))
            scale = float(DH) ** 0.25
            link(dve.memset(w_f[:, :], 1.0 / N))
            link.inc(dve.memset(w_f[0:DH, 0:1], 0.5 / N))
            link.inc(dve.memset(w_f[0:DH, 4:5], 0.5 / N))
            link.inc(dve.memset(w_f[DH:2 * DH, 4:5], scale ** 2 / N))
            link(dve.memset(w_f[2 * DH:2 * DH + 1, 4:5], scale ** 4 / N))
            dve.sem_inc(agg_added, 2)
            dve.sem_inc(y_used, 1)
            qk_h = st.qk.rearrange("p (g t e) -> p (g t) e", g=2 * H, t=T)
            nrm_h = st.nrm[:, :]

            def one_hot(s, c):
                dve.tensor_tensor(oh[:, c % RING], st.iota[:, :].unsqueeze(1).broadcast_to([P, SUP, P]),
                                  st.dloc[:, ds(s * SUP, SUP)].unsqueeze(2).broadcast_to([P, SUP, P]),
                                  ALU.is_equal).then_inc(oh_ready, 1)

            def add_sum(s, u, tile):
                dve.wait_ge(agg_done, s + 1 + RING)
                dve.wait_ge(agg_added, s + 2)
                out = st.x[:, ds(tile * D, D)]
                dve.tensor_tensor(out, out, p_agg[:, u, 0:D], ALU.add).then_inc(agg_added, 1)

            def products(b, which, g):
                src = kq[:, which, g * GT:(g + 1) * GT]
                a = src.ap
                shifted = bass.AP(src.tensor, src.offset, [a[0], [48, GT], [1, DH // 2 + 1], [1, DH]])
                out = feat[:, b, :, 0:QUAD].rearrange("p t (d e) -> p t d e", e=DH)
                dve.tensor_tensor(out, src[:, :, 0:DH].unsqueeze(2).broadcast_to([P, GT, DH // 2 + 1, DH]), shifted,
                                  ALU.mult).then_inc(f_ready, 1)
                dve.tensor_copy(feat[:, b, :, QUAD:QUAD + DH], src[:, :, 0:DH]).then_inc(f_ready, 1)

            def kq_head(which, h):
                g0 = (1 - which) * H + h
                link(dve.tensor_tensor(kq[:, which, :, 0:DH], qk_h[:, ds(g0 * T, T), :],
                                       nrm_h[:, ds(g0 * T, T)].unsqueeze(2).broadcast_to([P, T, DH]), ALU.mult))
                link(dve.tensor_copy(kq[:, which, :, DH:48], kq[:, which, :, 0:16]))

            def supers(h, g):
                for n in range(share[g]):
                    c = before[g] + n
                    s = h * PER_HEAD + c
                    tile = dve.value_load(st.tile_of[0:1, ds(s, 1)], min_val=0, max_val=T - 1)
                    one_hot(s + AHEAD, c + AHEAD)
                    add_sum(s, c % 2, tile)

            kq_head(0, 0)
            for c in range(AHEAD):
                one_hot(c, c)
            dve.wait_ge(f_used, 1)
            products(0, 0, 0)
            with link.loop(H, 4 + 1 + NG) as h:
                for g in range(2 * NG):
                    if g == NG - 2:
                        kq_head(1, h)
                    if g == 2 * NG - 2:
                        kq_head(0, (h + 1) % H)
                    dve.wait_ge(f_used, 2 * NG * h + g + 2)
                    n = (g + 1) % (2 * NG)
                    products(n % 2, n // NG, n % NG)
                    if g:
                        supers(h, g - 1)
                    if g >= NG:
                        y = g - NG
                        dve.wait_ge(y_ready, 2 + GT * (NG * h + y) + GT)
                        link(dve.reciprocal(r_y[:, :], p_y[:, :, DH]))
                        dve.tensor_tensor(st.mix[:, :].rearrange("p (t c) -> p t c", t=T)[:, y * GT:(y + 1) * GT, ds(h * DH, DH)],
                                          p_y[:, :, 0:DH], r_y[:, :].unsqueeze(2).broadcast_to([P, GT, DH]),
                                          ALU.mult).then_inc(y_used, 1)
                    if g == 2 * NG - 1:
                        supers(h, g)
                    if g == NG - 1:
                        dve.wait_ge(f_used, 2 * NG * h + NG + 2)
                        dve.tensor_tensor(kvs[:, 0:4], p_kv[:, 0:4], w_f[:, 0:4].unsqueeze(2).broadcast_to([P, 4, DH + 1]),
                                          ALU.mult).then_inc(kvs_ready, 1)
                        m = FS[4][1]
                        link(dve.tensor_scalar(kvs[0:m, 4], p_kv[0:m, 4], w_f[0:m, 4:5], None, ALU.mult))
                        dve.sem_inc(kvs_ready, 1)
            for c in range(TAIL):
                s = H * PER_HEAD + c
                tile = dve.value_load(st.tile_of[0:1, s:s + 1], min_val=0, max_val=T - 1)
                if s + AHEAD < NSUP:
                    one_hot(s + AHEAD, c + AHEAD)
                add_sum(s, c % 2, tile)

        @block.scalar
        def _(act):
            act.sem_inc(fT_ready, 2)
            with act.Fori(0, H) as h:
                for g in range(NG):
                    for j in range(GT):
                        n = GT * NG * h + GT * g + j
                        act.wait_ge(t_ready, n + 1)
                        act.wait_ge(y_ready, n + 1)
                        nc.scalar.copy(fT[:, j % 2, 0:4], p_ta[:, j % 2])
                        m = FS[4][1]
                        nc.scalar.copy(fT[0:m, j % 2, 4], p_tb[0:m, j % 2, 0:P]).then_inc(fT_ready, 1)

        @block.tensor
        def _(pe):
            pe.sem_inc(f_used, 2)
            pe.sem_inc(y_ready, 2)
            pe.sem_inc(agg_done, RING)

            def sums(s, c):
                pe.wait_ge(oh_ready, s + 1)
                pe.wait_ge(gathered[c % RING], 64 * ((s - c % RING) // RING + 1) if isinstance(s, int) else 64 * ring_turn(s, c))
                pe.wait_ge(agg_added, s + 1)
                for j in range(SUP):
                    last = pe.matmul(p_agg[:, c % 2, 0:D], oh[:, c % RING, j], rows[:, c % RING, j], start=j == 0, stop=j == SUP - 1)
                last.then_inc(agg_done, 1)

            turn = {}

            def ring_turn(s, c):
                return turn["h"] * (PER_HEAD // RING) + c // RING + 1

            def supers(h, g):
                turn["h"] = h
                for n in range(share[g]):
                    c = before[g] + n
                    sums(h * PER_HEAD + c, c)

            with pe.Fori(0, H) as h:
                for g in range(NG):
                    pe.wait_ge(f_ready, 2 * (2 * NG * h + g + 1))
                    b = g % 2
                    for j in range(GT):
                        v = st.v1[:, ds(h * (T * (DH + 1)) + (g * GT + j) * (DH + 1), DH + 1)]
                        for n, (f, m) in enumerate(FS):
                            last = pe.matmul(p_kv[0:m, n], feat[:, b, j, f:f + m], v, start=g == 0 and j == 0 and n == 0,
                                             stop=g == NG - 1 and j == GT - 1 and n == len(FS) - 1, skip_group_check=True)
                    last.then_inc(f_used, 1)
                    if g + 1 < NG:
                        supers(h, g)
                def turn_tile(g, j):
                    b = (NG + g) % 2
                    pe.wait_ge(fT_ready, GT * (NG * h + g) + j + 1)
                    for n in range(4):
                        pe.transpose(p_ta[:, j % 2, n], feat[:, b, j, n * P:(n + 1) * P], st.ident[:, :])
                    f, m = FS[4]
                    pe.transpose(p_tb[0:m, j % 2, 0:P], feat[:, b, j, f:f + m], st.ident[:, :]).then_inc(t_ready, 1)

                def y_tile(g, j):
                    pe.wait_ge(fT_ready, GT * (NG * h + g) + j + 3)
                    if j == 0:
                        pe.wait_ge(y_used, NG * h + g + 1)
                        if g == 0:
                            pe.wait_ge(kvs_ready, 2 * (h + 1))
                    for n, (f, m) in enumerate(FS):
                        last = pe.matmul(p_y[:, j], fT[0:m, j % 2, n], kvs[0:m, n], start=n == 0, stop=n == len(FS) - 1)
                    last.then_inc(y_ready, 1)

                def turn_first_tiles(g):
                    pe.wait_ge(f_ready, 2 * (2 * NG * h + NG + g + 1))
                    turn_tile(g, 0)
                    turn_tile(g, 1)

                turn_first_tiles(0)
                supers(h, NG - 1)
                for g in range(NG):
                    y_tile(g, 0)
                    turn_tile(g, 2)
                    y_tile(g, 1)
                    turn_tile(g, 3)
                    pe.drain().then_inc(f_used, 1)
                    y_tile(g, 2)
                    y_tile(g, 3)
                    if g + 1 < NG:
                        turn_first_tiles(g + 1)
                    supers(h, NG + g)
            for c in range(TAIL):
                sums(H * PER_HEAD + c, c)


def out0(nc, io, st):
    with ExitStack() as ctx:
        sb, ps, sem = tensors(nc, ctx)
        w_p = sb("w_p0", [P, K, D])
        b_a = sb("b_a0", [P, D])
        b_b = sb("b_b0", [P, D])
        a = sb("a0", [P, 2, D])
        aT = sb("aT0", [P, 2, D])
        p_t = ps("p_t0", [P, 2, 512])
        p_o = ps("p_o0", [P, 2, 512])
        w_in = sem("w_in0")
        dv = sem("dv3")
        a_ready = sem("a_ready0")
        held = sem("held0")
        transposed = sem("transposed0")
        aT_ready = sem("aT_ready0")
        o_ready = sem("o_ready0")
        o_used = sem("o_used0")
        block = ctx.enter_context(nc.Block())

        @block.sync
        def _(sp):
            sp.dma_start(w_p[:, :, :], io["wproj0"].rearrange("(k p) o -> p k o", p=P)).then_inc(w_in, 16)
            sp.dma_start(b_a[:, :], io["L0_mix_bproj"].partition_broadcast(P)).then_inc(w_in, 16)
            sp.dma_start(b_b[:, :], io["L0_gnn_bias_param"].partition_broadcast(P)).then_inc(w_in, 16)

        @block.gpsimd
        def _(pool):
            pool.sem_inc(a_ready, 2)
            with pool.Fori(0, T // 2) as i:
                for u in range(2):
                    t = 2 * i + u
                    hold(pool, transposed, t + 1, held)
                    pool.tensor_copy(a[:, u], st.mix[:, ds(t * D, D)]).then_inc(a_ready, 1)

        @block.vector
        def _(dve):
            link = Link(dve, dv)
            dve.wait_ge(w_in, 48)
            link(dve.tensor_tensor(b_a[:, :], b_a[:, :], b_b[:, :], ALU.add))
            x3 = st.x[:, :].rearrange("p (t d) -> p t d", t=T)
            link(dve.tensor_tensor(x3, x3, b_a[:, :].unsqueeze(1).broadcast_to([P, T, D]), ALU.add))
            dve.sem_inc(o_used, 2)
            with dve.Fori(0, T // 2) as i:
                for u in range(2):
                    t = 2 * i + u
                    dve.wait_ge(o_ready, t + 1)
                    out = st.x[:, ds(t * D, D)]
                    dve.tensor_tensor(out, out, p_o[:, u, 0:D], ALU.add).then_inc(o_used, 1)

        @block.scalar
        def _(act):
            act.sem_inc(aT_ready, 2)
            with act.Fori(0, T // 2) as i:
                for u in range(2):
                    t = 2 * i + u
                    act.wait_ge(transposed, t + 3)
                    act.wait_ge(o_used, t + 1)
                    nc.scalar.copy(aT[:, u], p_t[:, u, 0:D]).then_inc(aT_ready, 1)

        @block.tensor
        def _(pe):
            pe.wait_ge(w_in, 48)
            pe.sem_inc(transposed, 2)
            with pe.Fori(0, T // 2) as i:
                for u in range(2):
                    t = 2 * i + u
                    pe.wait_ge(a_ready, t + 3)
                    pe.wait_ge(aT_ready, t + 1)
                    for k in range(K):
                        last = pe.transpose(p_t[:, u, k * P:(k + 1) * P], a[:, u, k * P:(k + 1) * P], st.ident[:, :])
                    last.then_inc(transposed, 1)
                for u in range(2):
                    t = 2 * i + u
                    pe.wait_ge(aT_ready, t + 3)
                    pe.wait_ge(o_used, t + 1)
                    for k in range(K):
                        last = pe.matmul(p_o[:, u, 0:D], aT[:, u, k * P:(k + 1) * P], w_p[:, k], start=k == 0, stop=k == K - 1)
                    last.then_inc(o_ready, 1)


NE = 8


def normalise_and_route(nc, io, st, gate, bias, top2, tag):
    with ExitStack() as ctx:
        sb, ps, sem = tensors(nc, ctx)
        stats = sb("stats" + tag, [P, T * 6])
        mean = sb("mean" + tag, [P, T])
        sd = sb("sd" + tag, [P, T])
        rstd = sb("rstd" + tag, [P, T])
        xn = sb("xn" + tag, [P, 2, D])
        xT = sb("xT" + tag, [P, 2, D])
        w_g = sb("w_g" + tag, [P, K, NE])
        b_g = sb("b_g" + tag, [P, NE])
        lg = sb("lg" + tag, [P, T, NE])
        top = sb("top" + tag, [P, T])
        cand = sb("cand" + tag, [P, T, NE])
        rest = sb("rest" + tag, [P, T, NE])
        sel = sb("sel" + tag, [P, 2, T, NE])
        order = sb("order" + tag, [P, NE])
        p_t = ps("p_t" + tag, [P, 2, 512])
        p_g = ps("p_g" + tag, [P, 2, 512])
        w_in = sem("w_in" + tag)
        dv = sem("dv" + tag)
        ordered = sem("ordered" + tag)
        var_ready = sem("var_ready" + tag)
        sd_ready = sem("sd_ready" + tag)
        xn_ready = sem("xn_ready" + tag)
        transposed = sem("transposed" + tag)
        xT_ready = sem("xT_ready" + tag)
        g_ready = sem("g_ready" + tag)
        g_used = sem("g_used" + tag)
        lg_ready = sem("lg_ready" + tag)
        ex_ready = sem("ex_ready" + tag)
        block = ctx.enter_context(nc.Block())

        @block.sync
        def _(sp):
            sp.dma_start(w_g[:, :, :], io[gate].rearrange("(k p) o -> p k o", p=P)).then_inc(w_in, 16)
            sp.dma_start(b_g[:, :], io[bias].partition_broadcast(P)).then_inc(w_in, 16)

        @block.gpsimd
        def _(pool):
            pool.iota(order[:, :], pattern=[[-1, NE]], base=NE, channel_multiplier=0,
                      allow_small_or_imprecise_dtypes=True).then_inc(ordered, 1)

        @block.vector
        def _(dve):
            link = Link(dve, dv)
            layernorm_stats(dve, link, st, stats, mean, sd)
            dve.sem_inc(var_ready, 1)
            dve.wait_ge(sd_ready, 1)
            link(dve.reciprocal(rstd[:, :], sd[:, :]))
            dve.wait_ge(w_in, 32)
            dve.sem_inc(g_used, 2)

            def norm(t, u):
                dve.wait_ge(transposed, t + 1)
                dve.tensor_scalar(xn[:, u], st.x[:, ds(t * D, D)], mean[:, ds(t, 1)], rstd[:, ds(t, 1)],
                                  ALU.subtract, ALU.mult).then_inc(xn_ready, 1)

            def take(t, u):
                dve.wait_ge(g_ready, t + 1)
                dve.tensor_tensor(lg[:, :, :].rearrange("p t e -> p (t e)")[:, ds(t * NE, NE)], p_g[:, u, 0:NE],
                                  b_g[:, :], ALU.add).then_inc(g_used, 1)

            norm(0, 0)
            norm(1, 1)
            with dve.Fori(0, T // 2 - 1) as i:
                for u in range(2):
                    norm(2 * i + 2 + u, u)
                    take(2 * i + u, u)
            for u in range(2):
                take(T - 2 + u, u)
            dve.wait_ge(g_used, T + 2)
            wide = [P, T, NE]
            link(dve.tensor_reduce(top[:, :], lg[:, :, :], AX, ALU.max))
            link(dve.tensor_tensor(lg[:, :, :], lg[:, :, :], top[:, :].unsqueeze(2).broadcast_to(wide), ALU.subtract))
            dve.sem_inc(lg_ready, 1)
            dve.wait_ge(ex_ready, 1)
            link(dve.tensor_reduce(top[:, :], lg[:, :, :], AX, ALU.add))
            link(dve.reciprocal(top[:, :], top[:, :]))
            cw = st.cw[:, :].rearrange("p (t e) -> p t e", e=NE)
            link(dve.tensor_tensor(cw, lg[:, :, :], top[:, :].unsqueeze(2).broadcast_to(wide), ALU.mult))
            if top2:
                dve.wait_ge(ordered, 1)
                left = cw
                for n in range(2):
                    link(dve.tensor_reduce(top[:, :], left, AX, ALU.max))
                    link(dve.tensor_tensor(cand[:, :, :], left, top[:, :].unsqueeze(2).broadcast_to(wide), ALU.is_ge))
                    link(dve.tensor_tensor(cand[:, :, :], cand[:, :, :], order[:, :].unsqueeze(1).broadcast_to(wide), ALU.mult))
                    link(dve.tensor_reduce(top[:, :], cand[:, :, :], AX, ALU.max))
                    link(dve.tensor_tensor(sel[:, n], cand[:, :, :], top[:, :].unsqueeze(2).broadcast_to(wide), ALU.is_equal))
                    if n == 0:
                        link(dve.scalar_tensor_tensor(out=rest[:, :, :], in0=sel[:, 0], scalar=-4.0, in1=cw, op0=ALU.mult, op1=ALU.add))
                        left = rest[:, :, :]
                link(dve.tensor_tensor(sel[:, 0], sel[:, 0], sel[:, 1], ALU.add))
                link(dve.tensor_tensor(cw, cw, sel[:, 0], ALU.mult))

        @block.scalar
        def _(act):
            act.wait_ge(var_ready, 1)
            nc.scalar.activation(sd[:, :], sd[:, :], ACT.Sqrt).then_inc(sd_ready, 1)
            act.sem_inc(xT_ready, 2)
            with act.Fori(0, T // 2) as i:
                for u in range(2):
                    t = 2 * i + u
                    act.wait_ge(transposed, t + 3)
                    act.wait_ge(g_used, t + 1)
                    nc.scalar.copy(xT[:, u], p_t[:, u, 0:D])
                    nc.scalar.copy(st.xnT[:, :, ds(t * P, P)], p_t[:, u, 0:D].rearrange("p (k n) -> p k n", k=K)).then_inc(xT_ready, 1)
            act.wait_ge(lg_ready, 1)
            nc.scalar.activation(lg[:, :, :], lg[:, :, :], ACT.Exp).then_inc(ex_ready, 1)

        @block.tensor
        def _(pe):
            pe.sem_inc(transposed, 2)
            pe.wait_ge(w_in, 32)
            with pe.Fori(0, T // 2) as i:
                for u in range(2):
                    t = 2 * i + u
                    pe.wait_ge(xn_ready, t + 1)
                    pe.wait_ge(xT_ready, t + 1)
                    for k in range(K):
                        last = pe.transpose(p_t[:, u, k * P:(k + 1) * P], xn[:, u, k * P:(k + 1) * P], st.ident[:, :])
                    last.then_inc(transposed, 1)
                for u in range(2):
                    t = 2 * i + u
                    pe.wait_ge(xT_ready, t + 3)
                    pe.wait_ge(g_used, t + 1)
                    for k in range(K):
                        last = pe.matmul(p_g[:, u, 0:NE], xT[:, u, k * P:(k + 1) * P], w_g[:, k], start=k == 0, stop=k == K - 1)
                    last.then_inc(g_ready, 1)


HID0 = 512
HS = HID0 // P
BT = 4
NBLK = T // BT


def moe0(nc, io, st):
    with ExitStack() as ctx:
        sb, ps, sem = tensors(nc, ctx)
        hT = sb("hT", [P, 2, HS, BT * P])
        b1 = sb("b1m", [P, NE * HS])
        b2 = sb("b2m", [NE, D])
        cws = sb("cws", [P, BT * NE])
        cwT = sb("cwT", [NE, BT * P])
        p_h = ps("p_hm", [P, HS, 512])
        p_y = ps("p_ym", [P, 2, BT, D])
        b_in = sem("b_inm")
        cws_ready = sem("cws_ready")
        cwT_turned = sem("cwT_turned")
        cwT_ready = sem("cwT_ready")
        bias_ready = sem("bias_ready")
        bias_added = sem("bias_added")
        h_ready = sem("h_readym")
        hT_ready = sem("hT_ready")
        y_ready = sem("y_readym")
        y_used = sem("y_usedm")
        block = ctx.enter_context(nc.Block())

        @block.sync
        def _(sp):
            sp.dma_start(b1[:, :], io["moe_b1"]).then_inc(b_in, 16)
            sp.dma_start(b2[:, :], io["L0_ffn_b2"]).then_inc(b_in, 16)
            sp.wait_ge(b_in, 32)

        @block.vector
        def _(dve):
            dve.sem_inc(y_used, 2)
            with dve.Fori(0, NBLK) as i:
                dve.wait_ge(bias_ready, i + 1)
                dve.wait_ge(y_used, NE * i + 2)
                out = st.x[:, ds(i * BT * D, BT * D)]
                dve.tensor_tensor(out, out, p_h[:, 1:3].rearrange("p s n -> p (s n)"), ALU.add).then_inc(bias_added, 1)
                dve.wait_ge(bias_added, i + 1)
                for e in range(NE):
                    dve.wait_ge(y_ready, NE * i + e + 3)
                    dve.wait_ge(y_used, NE * i + e + 2)
                    for j in range(BT):
                        out = st.x[:, ds((i * BT + j) * D, D)]
                        last = dve.scalar_tensor_tensor(out=out, in0=p_y[:, e % 2, j], scalar=st.cw[:, ds((i * BT + j) * NE + e, 1)],
                                                        in1=out, op0=ALU.mult, op1=ALU.add)
                    last.then_inc(y_used, 1)

        @block.scalar
        def _(act):
            act.wait_ge(b_in, 32)
            with act.Fori(0, NBLK) as i:
                nc.scalar.copy(cws[:, :], st.cw[:, ds(i * BT * NE, BT * NE)]).then_inc(cws_ready, 1)
                act.wait_ge(cwT_turned, i + 1)
                nc.scalar.copy(cwT[:, :], p_h[0:NE, 0]).then_inc(cwT_ready, 1)
                for e in range(NE):
                    act.wait_ge(y_ready, NE * i + e + 1)
                    for s in range(HS):
                        act.wait_ge(h_ready, HS * (NE * i + e) + s + 1)
                        nc.scalar.activation(hT[:, e % 2, s], p_h[:, s], ACT.Gelu,
                                             bias=b1[:, e * HS + s:e * HS + s + 1]).then_inc(hT_ready, 1)

        @block.tensor
        def _(pe):
            pe.wait_ge(b_in, 32)
            pe.wait_ge(st.moe_w_in, 16 * 2 * NE)
            pe.sem_inc(y_ready, 2)
            with pe.Fori(0, NBLK) as i:
                pe.wait_ge(cws_ready, i + 1)
                for j in range(BT):
                    last = pe.transpose(p_h[0:NE, 0, j * P:(j + 1) * P], cws[:, j * NE:(j + 1) * NE], st.ident[:, :])
                last.then_inc(cwT_turned, 1)
                pe.wait_ge(cwT_ready, i + 1)
                for j in range(BT):
                    last = pe.matmul(p_h[:, 1 + j // 2, (j % 2) * D:(j % 2 + 1) * D], cwT[:, j * P:(j + 1) * P], b2[:, :],
                                     start=True, stop=True)
                last.then_inc(bias_ready, 1)

                def first(e):
                    for s in range(HS):
                        if e:
                            pe.wait_ge(hT_ready, HS * (NE * i + e - 1) + s + 1)
                        elif s == 1:
                            pe.wait_ge(bias_added, i + 1)
                        for k in range(K):
                            last = pe.matmul(p_h[:, s], st.w1[:, e, k, s * P:(s + 1) * P], st.xnT[:, k, ds(i * BT * P, BT * P)],
                                             start=k == 0, stop=k == K - 1)
                        last.then_inc(h_ready, 1)

                def second(e):
                    pe.wait_ge(hT_ready, HS * (NE * i + e + 1))
                    pe.wait_ge(y_used, NE * i + e + 1)
                    for j in range(BT):
                        for s in range(HS):
                            last = pe.matmul(p_y[:, e % 2, j], hT[:, e % 2, s, j * P:(j + 1) * P], st.w2[:, e, s],
                                             start=s == 0, stop=s == HS - 1)
                    last.then_inc(y_ready, 1)

                first(0)
                for e in range(NE):
                    if e + 1 < NE:
                        first(e + 1)
                    second(e)


def load_moe0(nc, io, st):
    with nc.Block() as block:
        @block.sync
        def _(sp):
            for e in range(NE):
                sp.dma_start(st.w1[:, e], io["L0_ffn_W1"][e].rearrange("(k p) o -> p k o", p=P)).then_inc(st.moe_w_in, 16)
                sp.dma_start(st.w2[:, e], io["L0_ffn_W2"][e].rearrange("(k p) o -> p k o", p=P)).then_inc(st.moe_w_in, 16)


HID1 = 64
HF = H * HID1
ROW1 = HF + H
LEAK = 0.2
S_RANGE = 40.0
UN = 6
assert NSUP % UN == 0


def front1(nc, io, st):
    with ExitStack() as ctx:
        sb, ps, sem = tensors(nc, ctx)
        stats = sb("stats1", [P, T * 6])
        mean = sb("mean1", [P, T])
        sd = sb("sd1", [P, T])
        rstd = sb("rstd1", [P, T])
        xn = sb("xn1", [P, 2, D])
        xT = sb("xT1", [P, 2, D])
        w_h = sb("w_h1", [P, K, HF])
        w_a = sb("w_a1", [P, K, 2 * H])
        a_b = sb("a_b1", [P, H, 2 * HID1])
        wa_t = sb("wa_t1", [P, K, HF])
        w_kv = sb("w_kv1", [P, K, 2 * D])
        w_q = sb("w_q1", [P, K, D])
        live = sb("live1", [P, T])
        row = sb("row1", [P, 2, ROW1])
        neg = sb("neg1", [P, 2, 2 * D])
        k_f = sb("k_f1", [P, 2, D])
        v_m = sb("v_m1", [P, 2, D + 1])
        context = sb("context1", [P, 2, D + 1])
        ends = sb("ends1", [P, 2 * H])
        end = sb("end1", [2 * H, 1])
        diag = sb("diag1", [2 * H, 2 * H])
        ones = sb("ones1", [2 * H, P])
        span = sb("span1", [P, H])
        widest = sb("widest1", [P, 1])
        z = sb("z1", [P, T, H])
        p_t = ps("p_t1", [P, 2, 512])
        p_h = ps("p_h1", [P, 512])
        p_kv = ps("p_kv1", [P, 512])
        p_q = ps("p_q1", [P, 512])
        p_c = ps("p_c1", [P, 2, 512])
        w_in = sem("w_in1")
        held = sem("held1")
        dv = sem("dv_front1")
        var_ready = sem("var_ready1")
        sd_ready = sem("sd_ready1")
        wa_ready = sem("wa_ready1")
        xn_ready = sem("xn_ready1")
        transposed = sem("transposed1")
        xT_ready = sem("xT_ready1")
        h_ready = sem("h_ready1")
        h_copied = sem("h_copied1")
        kv_ready = sem("kv_ready1")
        kv_used = sem("kv_used1")
        q_ready = sem("q_ready1")
        q_used = sem("q_used1")
        s_taken = sem("s_taken1")
        neg_ready = sem("neg_ready1")
        exp_ready = sem("exp_ready1")
        c_ready = sem("c_ready1")
        c_used = sem("c_used1")
        row_stored = sem("row_stored1")
        row_free = sem("row_free1")
        ends_ready = sem("ends_ready1")
        ends_turned = sem("ends_turned1")
        diag_ready = sem("diag_ready1")
        spread = sem("spread1")
        z_asked = sem("z_asked1")
        z_ready = sem("z_ready1")
        z_stored = sem("z_stored1")
        block = ctx.enter_context(nc.Block())

        @block.sync
        def _(sp):
            sp.dma_start(w_h[:, :, :], io["gat_w"].rearrange("(k p) o -> p k o", p=P)).then_inc(w_in, 16)
            sp.dma_start(a_b[:, :, :], io["L1_gnn_a"].rearrange("h o -> (h o)").partition_broadcast(P)).then_inc(w_in, 16)
            sp.dma_start(w_kv[:, :, :], io["wkv1"].rearrange("(k p) o -> p k o", p=P)).then_inc(w_in, 16)
            sp.dma_start(w_q[:, :, :], io["wq1"].rearrange("(k p) o -> p k o", p=P)).then_inc(w_in, 16)
            sp.sem_inc(row_free, 2)
            with sp.Fori(0, T // 2) as i:
                for u in range(2):
                    t = 2 * i + u
                    hold(sp, h_copied, t + 2, held)
                    hold(sp, s_taken, t + 1, held)
                    sp.dma_start(st.g_table[ds(t * P, P), :], row[:, u]).then_inc(row_stored, 16)
                    sp.wait_ge(row_stored, (t + 1) * 16)
                    sp.sem_inc(row_free, 1)
            sp.wait_ge(z_ready, 1)
            sp.dma_start(st.z_table.rearrange("(t p) h -> p t h", p=P), z[:, :, :]).then_inc(z_stored, 16)
            sp.wait_ge(z_stored, 16)

        @block.vector
        def _(dve):
            link = Link(dve, dv)
            layernorm_stats(dve, link, st, stats, mean, sd)
            dve.sem_inc(var_ready, 1)
            dve.wait_ge(w_in, 64)
            for side in range(2):
                part = a_b[:, :, side * HID1:(side + 1) * HID1]
                for k in range(K):
                    link(dve.tensor_tensor(wa_t[:, k].rearrange("p (h o) -> p h o", h=H),
                                           w_h[:, k].rearrange("p (h o) -> p h o", h=H), part, ALU.mult))
                    link(dve.tensor_reduce(w_a[:, k, side * H:(side + 1) * H], wa_t[:, k].rearrange("p (h o) -> p h o", h=H),
                                           AX, ALU.add))
            dve.sem_inc(wa_ready, 1)
            dve.wait_ge(sd_ready, 1)
            link(dve.reciprocal(rstd[:, :], sd[:, :]))
            link(dve.memset(live[:, :], 1.0))
            link(dve.tensor_copy(live[:, T - 1:T], st.rowmask[:, :]))
            link(dve.memset(context[:, :, :], 0.0))
            link(dve.memset(st.cb[:, :, :], 0.0))
            link(dve.memset(ones[:, :], 1.0))
            link(dve.memset(k_f[:, 1], 0.0))
            link(dve.memset(v_m[:, 1], 0.0))
            dve.sem_inc(kv_used, 1)
            dve.sem_inc(q_used, 1)
            dve.sem_inc(c_used, 1)

            def norm(t, u):
                dve.wait_ge(transposed, t + 1)
                dve.tensor_scalar(xn[:, u], st.x[:, ds(t * D, D)], mean[:, ds(t, 1)], rstd[:, ds(t, 1)],
                                  ALU.subtract, ALU.mult).then_inc(xn_ready, 1)

            def take(t, u):
                dve.wait_ge(kv_ready, t + 1)
                dve.tensor_scalar(neg[:, u, 0:D], p_kv[:, 0:D], 0.0, None, ALU.min)
                link.inc(dve.tensor_scalar(v_m[:, u, 0:D], p_kv[:, D:], live[:, ds(t, 1)], None, ALU.mult))
                link.inc(dve.tensor_copy(v_m[:, u, D:D + 1], live[:, ds(t, 1)]))
                dve.wait_ge(q_ready, t + 1)
                dve.tensor_scalar(neg[:, u, D:], p_q[:, 0:D], 0.0, None, ALU.min).then_inc(neg_ready, 1)
                dve.wait_ge(row_free, t + 1)
                dve.tensor_copy(row[:, u, HF:], p_q[:, D:D + H])
                dve.tensor_copy(st.s_all[:, ds(t * 2 * H, 2 * H)], p_q[:, D:D + 2 * H]).then_inc(s_taken, 1)
                dve.wait_ge(exp_ready, t + 1)
                dve.scalar_tensor_tensor(out=k_f[:, u], in0=p_kv[:, 0:D], scalar=0.0, in1=neg[:, u, 0:D],
                                         op0=ALU.max, op1=ALU.add).then_inc(kv_used, 1)
                dve.scalar_tensor_tensor(out=st.qT[:, ds(t * D, D)], in0=p_q[:, 0:D], scalar=0.0, in1=neg[:, u, D:],
                                         op0=ALU.max, op1=ALU.add).then_inc(q_used, 1)
                add_context(t)

            def add_context(t):
                dve.wait_ge(c_ready, t + 1)
                dve.wait_ge(c_used, t + 1)
                dve.tensor_tensor(context[:, :, :], context[:, :, :], p_c[:, :, 0:D + 1], ALU.add).then_inc(c_used, 1)

            norm(0, 0)
            norm(1, 1)
            with link.loop(T // 2 - 1, 4) as i:
                for u in range(2):
                    norm(2 * i + 2 + u, u)
                    take(2 * i + u, u)
            for u in range(2):
                take(T - 2 + u, u)
            add_context(T)
            dve.wait_ge(c_used, T + 2)
            dve.wait_ge(s_taken, T)
            dve.wait_ge(dv, link.base + link.k)
            for g in range(4):
                r = slice(g * DH, (g + 1) * DH)
                for c in range(2):
                    link.inc(dve.tensor_copy(st.cb[r, c, g * DH:(g + 1) * DH], context[r, c, (4 * c + g) * DH:(4 * c + g + 1) * DH]))
                    link.inc(dve.tensor_copy(st.cb[r, c, P + g:P + g + 1], context[r, c, D:D + 1]))
            s3 = st.s_all[:, :].rearrange("p (t c) -> p c t", t=T)[:, 0:H, :]
            link.inc(dve.tensor_reduce(ends[:, 0:H], s3, AX, ALU.max))
            link(dve.tensor_reduce(span[:, :], s3, AX, ALU.min))
            link(dve.tensor_scalar(ends[:, H:], span[:, :], -1.0, None, ALU.mult))
            dve.sem_inc(ends_ready, 1)
            dve.wait_ge(ends_turned, 1)
            link(dve.tensor_reduce(end[:, :], p_q[0:2 * H, 0:P], AX, ALU.max))
            link(dve.tensor_scalar(diag[:, :], st.ident[0:2 * H, 0:2 * H], end[:, 0:1], None, ALU.mult))
            dve.sem_inc(diag_ready, 1)
            dve.wait_ge(spread, 1)
            link(dve.tensor_copy(ends[:, :], p_c[:, 0, 0:2 * H]))
            link.inc(dve.tensor_copy(st.s_max[:, :], ends[:, 0:H]))
            link(dve.tensor_tensor(span[:, :], ends[:, 0:H], ends[:, H:], ALU.add))
            link(dve.tensor_scalar(st.s_unit[:, :], span[:, :], 1.0 / S_RANGE, 1.0, ALU.mult, ALU.max))
            link(dve.tensor_reduce(widest[:, :], span[:, :], AX, ALU.max))
            link(dve.tensor_scalar(st.wide_flag[:, :], widest[:, :], S_RANGE, None, ALU.is_gt))
            link(dve.reciprocal(span[:, :], st.s_unit[:, :]))
            wide = [P, T, H]
            sv = st.s_all[:, :].rearrange("p (t c) -> p t c", t=T)[:, :, 0:H]
            link(dve.tensor_tensor(z[:, :, :], sv, st.s_max[:, :].unsqueeze(1).broadcast_to(wide), ALU.subtract))
            link(dve.tensor_tensor(z[:, :, :], z[:, :, :], span[:, :].unsqueeze(1).broadcast_to(wide), ALU.mult))
            dve.sem_inc(z_asked, 1)

        @block.scalar
        def _(act):
            act.wait_ge(var_ready, 1)
            nc.scalar.activation(sd[:, :], sd[:, :], ACT.Sqrt).then_inc(sd_ready, 1)
            act.sem_inc(xT_ready, 2)
            act.sem_inc(h_copied, 1)
            with act.Fori(0, T // 2) as i:
                for u in range(2):
                    t = 2 * i + u
                    act.wait_ge(transposed, t + 3)
                    nc.scalar.copy(xT[:, u], p_t[:, u, 0:D]).then_inc(xT_ready, 1)
                for u in range(2):
                    t = 2 * i + u
                    act.wait_ge(neg_ready, t + 1)
                    nc.scalar.activation(neg[:, u], neg[:, u], ACT.Exp).then_inc(exp_ready, 1)
                    act.wait_ge(h_ready, t + 1)
                    act.wait_ge(row_free, t + 1)
                    nc.scalar.copy(row[:, u, 0:HF], p_h[:, :]).then_inc(h_copied, 1)
            act.wait_ge(z_asked, 1)
            nc.scalar.activation(z[:, :, :], z[:, :, :], ACT.Exp).then_inc(z_ready, 1)

        @block.tensor
        def _(pe):
            pe.wait_ge(w_in, 64)
            pe.wait_ge(wa_ready, 1)
            pe.sem_inc(transposed, 2)

            def context_product(t, u):
                pe.wait_ge(kv_used, t + 1)
                pe.wait_ge(c_used, t + 1)
                for c in range(2):
                    last = pe.matmul(p_c[:, c, 0:D + 1], k_f[:, 1 - u, c * P:(c + 1) * P], v_m[:, 1 - u], start=True, stop=True)
                last.then_inc(c_ready, 1)

            with pe.Fori(0, T // 2) as i:
                for u in range(2):
                    t = 2 * i + u
                    pe.wait_ge(xn_ready, t + 1)
                    pe.wait_ge(xT_ready, t + 1)
                    for k in range(K):
                        last = pe.transpose(p_t[:, u, k * P:(k + 1) * P], xn[:, u, k * P:(k + 1) * P], st.ident[:, :])
                    last.then_inc(transposed, 1)
                for u in range(2):
                    t = 2 * i + u
                    pe.wait_ge(xT_ready, t + 3)
                    halves = [xT[:, u, k * P:(k + 1) * P] for k in range(K)]
                    pe.wait_ge(kv_used, t + 1)
                    for k in range(K):
                        last = pe.matmul(p_kv[:, :], halves[k], w_kv[:, k], start=k == 0, stop=k == K - 1)
                    last.then_inc(kv_ready, 1)
                    pe.wait_ge(q_used, t + 1)
                    for c in range(2):
                        for k in range(K):
                            pe.matmul(p_q[:, c * P:(c + 1) * P], w_q[:, k, c * P:(c + 1) * P], halves[k], start=k == 0, stop=k == K - 1)
                    for k in range(K):
                        last = pe.matmul(p_q[:, D:D + 2 * H], halves[k], w_a[:, k], start=k == 0, stop=k == K - 1)
                    last.then_inc(q_ready, 1)
                    context_product(t, u)
                    pe.wait_ge(h_copied, t + 1)
                    for k in range(K):
                        last = pe.matmul(p_h[:, :], halves[k], w_h[:, k], start=k == 0, stop=k == K - 1)
                    last.then_inc(h_ready, 1)
            context_product(T, T % 2)
            pe.wait_ge(ends_ready, 1)
            pe.transpose(p_q[0:2 * H, 0:P], ends[:, :], st.ident[:, :]).then_inc(ends_turned, 1)
            pe.wait_ge(diag_ready, 1)
            pe.matmul(p_c[:, 0, 0:2 * H], ones[:, :], diag[:, :], start=True, stop=True).then_inc(spread, 1)


def segment_bound(nc, io, st):
    RING = 3
    with ExitStack() as ctx:
        sb, ps, sem = tensors(nc, ctx)
        rows = sb("rows_z", [P, RING, SUP, H])
        idx = sb("idx_z", [P, RING, SUP], I32)
        oh = sb("oh_z", [P, 2, SUP, P])
        zsum = sb("zsum", [P, T * H])
        p_z = ps("p_z", [P, 2, 512])
        cleared = sem("cleared_z")
        idx_ready = sem("idx_ready_z")
        held = sem("held_z")
        oh_ready = sem("oh_ready_z")
        agg_done = sem("agg_done_z")
        agg_added = sem("agg_added_z")
        gathered = [sem(f"gathered_z{r}") for r in range(RING)]
        dv = sem("dv_z")
        sum_ready = sem("sum_ready")
        ln_ready = sem("ln_ready")
        block = ctx.enter_context(nc.Block())

        @block.gpsimd
        def _(pool):
            wide = pool.value_load(st.wide_flag[0:1, 0:1], min_val=0, max_val=1)
            with pool.If(wide > 0):
                with pool.Fori(0, NSUP // UN) as i:
                    for c in range(UN):
                        s, r = i * UN + c, c % RING
                        hold(pool, agg_done, s + 1, held)
                        pool.tensor_copy(idx[:, r], st.row_src[:, ds(s * SUP, SUP)]).then_inc(idx_ready, 1)
                        hold(pool, idx_ready, s + 1, held)
                        for j in range(SUP):
                            pool.indirect_dma_start(rows[:, r, j], None, st.z_table,
                                                    bass.IndirectOffsetOnAxis(ap=idx[:, r, j:j + 1], axis=0)).then_inc(gathered[r], 16)

        @block.vector
        def _(dve):
            link = Link(dve, dv)
            link(dve.memset(zsum[:, :], 0.0))

            def one_hot(s, u):
                dve.wait_ge(agg_done, s + 2)
                dve.tensor_tensor(oh[:, u], st.iota[:, :].unsqueeze(1).broadcast_to([P, SUP, P]),
                                  st.dloc[:, ds(s * SUP, SUP)].unsqueeze(2).broadcast_to([P, SUP, P]),
                                  ALU.is_equal).then_inc(oh_ready, 1)

            wide = dve.value_load(st.wide_flag[0:1, 0:1], min_val=0, max_val=1)
            with dve.If(wide > 0):
                dve.sem_inc(agg_added, 2)
                one_hot(0, 0)
                with dve.Fori(0, NSUP // UN) as i:
                    for c in range(UN):
                        s = i * UN + c
                        one_hot(s + 1, (c + 1) % 2)
                        tile = dve.value_load(st.tile_of[0:1, ds(s, 1)], min_val=0, max_val=T - 1)
                        dve.wait_ge(agg_done, s + 4)
                        dve.wait_ge(agg_added, s + 2)
                        out = zsum[:, ds(tile * H, H)]
                        dve.tensor_tensor(out, out, p_z[:, c % 2, 0:H], ALU.add).then_inc(agg_added, 1)
                dve.wait_ge(agg_added, NSUP + 2)
                dve.tensor_scalar(zsum[:, :], zsum[:, :], 2.0 ** -62, None, ALU.max).then_inc(sum_ready, 1)
                dve.wait_ge(ln_ready, 1)
            wide_by = [P, T, H]
            z3 = zsum[:, :].rearrange("p (t h) -> p t h", t=T)
            s3 = st.s_all[:, :].rearrange("p (t c) -> p t c", t=T)
            link(dve.tensor_tensor(z3, z3, st.s_unit[:, :].unsqueeze(1).broadcast_to(wide_by), ALU.mult))
            link(dve.tensor_tensor(z3, z3, st.s_max[:, :].unsqueeze(1).broadcast_to(wide_by), ALU.add))
            link(dve.tensor_tensor(z3, z3, s3[:, :, H:], ALU.add))
            link(dve.tensor_copy(s3[:, :, 0:H], s3[:, :, H:]))
            link(dve.scalar_tensor_tensor(out=s3[:, :, H:], in0=z3, scalar=LEAK, in1=z3, op0=ALU.mult, op1=ALU.max))

        @block.scalar
        def _(act):
            wide = act.value_load(st.wide_flag[0:1, 0:1], min_val=0, max_val=1)
            with act.If(wide > 0):
                act.wait_ge(sum_ready, 1)
                nc.scalar.activation(zsum[:, :], zsum[:, :], ACT.Ln).then_inc(ln_ready, 1)

        @block.tensor
        def _(pe):
            wide = pe.value_load(st.wide_flag[0:1, 0:1], min_val=0, max_val=1)
            with pe.If(wide > 0):
                pe.sem_inc(agg_done, 3)
                with pe.Fori(0, NSUP // UN) as i:
                    for c in range(UN):
                        s, r = i * UN + c, c % RING
                        pe.wait_ge(oh_ready, s + 1)
                        pe.wait_ge(gathered[r], 64 * (2 * i + c // RING + 1))
                        pe.wait_ge(agg_added, s + 1)
                        for j in range(SUP):
                            last = pe.matmul(p_z[:, c % 2, 0:H], oh[:, c % 2, j], rows[:, r, j], start=j == 0, stop=j == SUP - 1)
                        last.then_inc(agg_done, 1)


def attend(nc, io, st):
    RING = 6
    with ExitStack() as ctx:
        sb, ps, sem = tensors(nc, ctx)
        rows = sb("rows_g", [P, RING, SUP, ROW1])
        idx = sb("idx_g", [P, RING, SUP], I32)
        oh = sb("oh_g", [P, RING, SUP, P])
        ohT = sb("ohT_g", [P, 2, SUP, P])
        node = sb("node_g", [P, 2, 2 * H])
        score = sb("score_g", [P, 2, SUP, H])
        p_ot = ps("p_ot", [P, 2, SUP, P])
        p_n = ps("p_n", [P, 2, 512])
        p_a = ps("p_ag", [P, 2, 512])
        p_d = ps("p_dg", [P, 2, 512])
        dv = sem("dv_g")
        idx_ready = sem("idx_ready_g")
        held = sem("held_g")
        oh_ready = sem("oh_ready_g")
        ot_ready = sem("ot_ready")
        ohT_ready = sem("ohT_ready")
        n_ready = sem("n_ready")
        score_ready = sem("score_ready")
        ex_ready = sem("ex_ready_g")
        msg_ready = sem("msg_ready")
        agg_done = sem("agg_done_g")
        agg_added = sem("agg_added_g")
        gathered = [sem(f"gathered_g{r}") for r in range(RING)]
        block = ctx.enter_context(nc.Block())

        def every_super(eng, loop, step):
            for c in range(2):
                step(c, c, 0)
            with loop as i:
                for c in range(2, UN + 2):
                    step(i * UN + c, c, i)
            for c in range(2, UN):
                step(NSUP - UN + c, c, NSUP // UN - 1)

        @block.gpsimd
        def _(pool):
            with pool.Fori(0, NSUP // UN) as i:
                for c in range(UN):
                    s, r = i * UN + c, c % RING
                    hold(pool, agg_done, s + 1, held)
                    pool.tensor_copy(idx[:, r], st.row_src[:, ds(s * SUP, SUP)]).then_inc(idx_ready, 1)
                    hold(pool, idx_ready, s + 1, held)
                    for j in range(SUP):
                        pool.indirect_dma_start(rows[:, r, j], None, st.g_table,
                                                bass.IndirectOffsetOnAxis(ap=idx[:, r, j:j + 1], axis=0)).then_inc(gathered[r], 16)

        @block.vector
        def _(dve):
            link = Link(dve, dv)

            def one_hot(s, c):
                dve.tensor_tensor(oh[:, c % RING], st.iota[:, :].unsqueeze(1).broadcast_to([P, SUP, P]),
                                  st.dloc[:, ds(s * SUP, SUP)].unsqueeze(2).broadcast_to([P, SUP, P]),
                                  ALU.is_equal).then_inc(oh_ready, 1)

            def add_sum(s, c):
                tile = dve.value_load(st.tile_of[0:1, ds(s, 1)], min_val=0, max_val=T - 1)
                dve.wait_ge(agg_done, s + 1 + RING)
                dve.wait_ge(agg_added, s + 2)
                out = st.acc[:, ds(tile * ROW1, HF)]
                dve.tensor_tensor(out, out, p_a[:, c % 2], ALU.add)
                out = st.acc[:, ds(tile * ROW1 + HF, H)]
                dve.tensor_tensor(out, out, p_d[:, c % 2, 0:H], ALU.add).then_inc(agg_added, 1)

            def step(s, c, i):
                u, r = c % 2, c % RING
                dve.wait_ge(n_ready, s + 1)
                dve.wait_ge(gathered[r], 64 * (i + c // RING + 1))
                n = p_n[:, u, 0:SUP * 2 * H].rearrange("p (j c) -> p j c", j=SUP)
                link(dve.tensor_tensor(score[:, u], rows[:, r, :, HF:], n[:, :, 0:H], ALU.add))
                link(dve.scalar_tensor_tensor(out=score[:, u], in0=score[:, u], scalar=LEAK, in1=score[:, u],
                                              op0=ALU.mult, op1=ALU.max))
                dve.tensor_tensor(score[:, u], score[:, u], n[:, :, H:], ALU.subtract).then_inc(score_ready, 1)
                if not isinstance(s, int) or s + 2 < NSUP:
                    one_hot(s + 2, c + 2)
                if not isinstance(s, int) or s >= 2:
                    add_sum(s - 2, c - 2)
                dve.wait_ge(ex_ready, s + 1)
                feats = rows[:, r, :, 0:HF].rearrange("p j (h o) -> p j h o", h=H)
                dve.tensor_tensor(feats, feats, rows[:, r, :, HF:].unsqueeze(3).broadcast_to([P, SUP, H, HID1]),
                                  ALU.mult).then_inc(msg_ready, 1)

            link(dve.memset(st.acc[:, :], 0.0))
            dve.sem_inc(agg_added, 2)
            one_hot(0, 0)
            one_hot(1, 1)
            every_super(dve, link.loop(NSUP // UN - 1, 2 * UN), step)
            add_sum(NSUP - 2, NSUP - 2)
            add_sum(NSUP - 1, NSUP - 1)

        @block.scalar
        def _(act):
            def turn(s, c):
                tile = act.value_load(st.tile_of[0:1, ds(s, 1)], min_val=0, max_val=T - 1)
                nc.scalar.copy(node[:, c % 2], st.s_all[:, ds(tile * 2 * H, 2 * H)])
                act.wait_ge(ot_ready, s + 1)
                nc.scalar.copy(ohT[:, c % 2], p_ot[:, c % 2]).then_inc(ohT_ready, 1)

            def step(s, c, i):
                act.wait_ge(score_ready, s + 1)
                nc.scalar.activation(rows[:, c % RING, :, HF:], score[:, c % 2], ACT.Exp).then_inc(ex_ready, 1)
                if not isinstance(s, int) or s + 2 < NSUP:
                    turn(s + 2, c + 2)

            turn(0, 0)
            turn(1, 1)
            every_super(act, act.Fori(0, NSUP // UN - 1), step)

        @block.tensor
        def _(pe):
            pe.sem_inc(agg_done, RING)

            def turn(s, c):
                pe.wait_ge(oh_ready, s + 1)
                for j in range(SUP):
                    last = pe.transpose(p_ot[:, c % 2, j], oh[:, c % RING, j], st.ident[:, :])
                last.then_inc(ot_ready, 1)

            def spread(s, c):
                pe.wait_ge(ohT_ready, s + 1)
                for j in range(SUP):
                    last = pe.matmul(p_n[:, c % 2, j * 2 * H:(j + 1) * 2 * H], ohT[:, c % 2, j], node[:, c % 2], start=True, stop=True)
                last.then_inc(n_ready, 1)

            def step(s, c, i):
                r = c % RING
                if not isinstance(s, int) or s + 2 < NSUP:
                    turn(s + 2, c + 2)
                if not isinstance(s, int) or s + 1 < NSUP:
                    spread(s + 1, c + 1)
                pe.wait_ge(msg_ready, s + 1)
                pe.wait_ge(agg_added, s + 1)
                for j in range(SUP):
                    pe.matmul(p_a[:, c % 2], oh[:, r, j], rows[:, r, j, 0:HF], start=j == 0, stop=j == SUP - 1)
                    last = pe.matmul(p_d[:, c % 2, 0:H], oh[:, r, j], rows[:, r, j, HF:], start=j == 0, stop=j == SUP - 1)
                last.then_inc(agg_done, 1)

            turn(0, 0)
            turn(1, 1)
            spread(0, 0)
            every_super(pe, pe.Fori(0, NSUP // UN - 1), step)


def out1(nc, io, st):
    with ExitStack() as ctx:
        sb, ps, sem = tensors(nc, ctx)
        w_o = sb("w_o", [P, HF // P, D])
        w_p = sb("w_p1", [P, K, D])
        b_o = sb("b_o", [P, D])
        b_p = sb("b_p", [P, D])
        den = sb("den", [P, T, H])
        on = sb("on", [P, 2, HF])
        onT = sb("onT", [P, 2, HF])
        q_s = sb("q_s", [P, 2, D])
        d_m = sb("d_m", [P, 2, H])
        at = sb("at", [P, 2, D])
        atT = sb("atT", [P, 2, D])
        y = sb("y_o", [P, 2, D])
        yn = sb("yn_o", [P, 2, D])
        p_t = ps("p_to", [P, 2, 512])
        p_m = ps("p_mo", [P, 2, 512])
        p_s = ps("p_so", [P, 2, 512])
        p_o = ps("p_oo", [P, 2, 512])
        w_in = sem("w_ino")
        dv = sem("dvo")
        on_ready = sem("on_ready")
        on_turned = sem("on_turned")
        onT_ready = sem("onT_ready")
        q_ready = sem("q_ready_o")
        m_ready = sem("m_ready")
        at_ready = sem("at_ready")
        at_turned = sem("at_turned")
        atT_ready = sem("atT_ready")
        o_ready = sem("o_ready1")
        o_used = sem("o_used1")
        e_asked = sem("e_asked")
        e_ready = sem("e_ready")
        block = ctx.enter_context(nc.Block())

        @block.sync
        def _(sp):
            sp.dma_start(w_o[:, :, :], io["L1_gnn_Wo"].rearrange("(k p) o -> p k o", p=P)).then_inc(w_in, 16)
            sp.dma_start(w_p[:, :, :], io["wproj1"].rearrange("(k p) o -> p k o", p=P)).then_inc(w_in, 16)
            sp.dma_start(b_o[:, :], io["L1_gnn_bo"].partition_broadcast(P)).then_inc(w_in, 16)
            sp.dma_start(b_p[:, :], io["L1_mix_bproj"].partition_broadcast(P)).then_inc(w_in, 16)
            sp.wait_ge(w_in, 64)

        @block.vector
        def _(dve):
            link = Link(dve, dv)
            acc = st.acc[:, :].rearrange("p (t r) -> p t r", t=T)
            link(dve.tensor_scalar(den[:, :, :], acc[:, :, HF:], 1e-30, None, ALU.max))
            link(dve.reciprocal(den[:, :, :], den[:, :, :]))
            dve.wait_ge(w_in, 64)
            x3 = st.x[:, :].rearrange("p (t d) -> p t d", t=T)
            link(dve.tensor_tensor(x3, x3, b_p[:, :].unsqueeze(1).broadcast_to([P, T, D]), ALU.add))
            dve.sem_inc(o_used, 2)
            dflat = den[:, :, :].rearrange("p t h -> p (t h)")

            def early(t, u):
                dve.wait_ge(on_turned, t + 1)
                dve.tensor_tensor(on[:, u].rearrange("p (h o) -> p h o", h=H),
                                  st.acc[:, ds(t * ROW1, HF)].rearrange("p (h o) -> p h o", h=H),
                                  dflat[:, ds(t * H, H)].unsqueeze(2).broadcast_to([P, H, HID1]), ALU.mult).then_inc(on_ready, 1)

            def middle(t, u):
                dve.wait_ge(m_ready, t + 1)
                m = p_m[:, u, 0:2 * (P + 4)].rearrange("p (c n) -> p c n", c=2)
                d = d_m[:, u].rearrange("p (c g) -> p c g", c=2)
                link(dve.tensor_scalar(d, m[:, :, P:], 1e-6, None, ALU.max))
                link(dve.reciprocal(d_m[:, u], d_m[:, u]))
                dve.wait_ge(at_turned, t + 1)
                for c in range(2):
                    last = dve.tensor_tensor(at[:, u, c * P:(c + 1) * P].rearrange("p (g e) -> p g e", g=4),
                                             m[:, c, 0:P].rearrange("p (g e) -> p g e", g=4),
                                             d[:, c].unsqueeze(2).broadcast_to([P, 4, DH]), ALU.mult)
                last.then_inc(at_ready, 1)

            def ask(t, u):
                dve.wait_ge(o_ready, t + 1)
                link(dve.tensor_tensor(y[:, u], p_o[:, u, 0:D], b_o[:, :], ALU.add))
                link.inc(dve.tensor_tensor(st.x[:, ds(t * D, D)], st.x[:, ds(t * D, D)], p_o[:, u, D:], ALU.add))
                dve.tensor_scalar(yn[:, u], y[:, u], 0.0, None, ALU.min).then_inc(e_asked, 1)

            def late(t, u):
                dve.wait_ge(e_ready, t + 1)
                link(dve.scalar_tensor_tensor(out=y[:, u], in0=y[:, u], scalar=0.0, in1=yn[:, u], op0=ALU.max, op1=ALU.add))
                dve.scalar_tensor_tensor(out=st.x[:, ds(t * D, D)], in0=y[:, u], scalar=-1.0, in1=st.x[:, ds(t * D, D)],
                                         op0=ALU.add, op1=ALU.add).then_inc(o_used, 1)

            for u in range(2):
                early(u, u)
            with link.loop(T // 2 - 1, 10) as i:
                for u in range(2):
                    middle(2 * i + u, u)
                for u in range(2):
                    early(2 * i + 2 + u, u)
                for u in range(2):
                    ask(2 * i + u, u)
                for u in range(2):
                    late(2 * i + u, u)
            for stage in (middle, ask, late):
                for u in range(2):
                    stage(T - 2 + u, u)

        @block.scalar
        def _(act):
            act.sem_inc(q_ready, 2)
            act.sem_inc(onT_ready, 2)
            act.sem_inc(atT_ready, 2)
            with act.Fori(0, T // 2) as i:
                for u in range(2):
                    t = 2 * i + u
                    nc.scalar.copy(q_s[:, u], st.qT[:, ds(t * D, D)]).then_inc(q_ready, 1)
                    act.wait_ge(on_turned, t + 3)
                    nc.scalar.copy(onT[:, u], p_t[:, u]).then_inc(onT_ready, 1)
                for u in range(2):
                    t = 2 * i + u
                    act.wait_ge(at_turned, t + 3)
                    nc.scalar.copy(atT[:, u], p_s[:, u, 0:D]).then_inc(atT_ready, 1)
                for u in range(2):
                    t = 2 * i + u
                    act.wait_ge(e_asked, t + 1)
                    nc.scalar.activation(yn[:, u], yn[:, u], ACT.Exp).then_inc(e_ready, 1)

        @block.tensor
        def _(pe):
            pe.wait_ge(w_in, 64)
            pe.sem_inc(on_turned, 2)
            pe.sem_inc(at_turned, 2)
            with pe.Fori(0, T // 2) as i:
                for u in range(2):
                    t = 2 * i + u
                    pe.wait_ge(q_ready, t + 3)
                    for c in range(2):
                        last = pe.matmul(p_m[:, u, c * (P + 4):(c + 1) * (P + 4)], q_s[:, u, c * P:(c + 1) * P], st.cb[:, c],
                                         start=True, stop=True)
                    last.then_inc(m_ready, 1)
                    pe.wait_ge(on_ready, t + 1)
                    pe.wait_ge(onT_ready, t + 1)
                    for k in range(HF // P):
                        last = pe.transpose(p_t[:, u, k * P:(k + 1) * P], on[:, u, k * P:(k + 1) * P], st.ident[:, :])
                    last.then_inc(on_turned, 1)
                for u in range(2):
                    t = 2 * i + u
                    pe.wait_ge(at_ready, t + 1)
                    for k in range(K):
                        last = pe.transpose(p_s[:, u, k * P:(k + 1) * P], at[:, u, k * P:(k + 1) * P], st.ident[:, :])
                    last.then_inc(at_turned, 1)
                for u in range(2):
                    t = 2 * i + u
                    pe.wait_ge(onT_ready, t + 3)
                    pe.wait_ge(o_used, t + 1)
                    for k in range(HF // P):
                        pe.matmul(p_o[:, u, 0:D], onT[:, u, k * P:(k + 1) * P], w_o[:, k], start=k == 0, stop=k == HF // P - 1)
                    pe.wait_ge(atT_ready, t + 3)
                    for k in range(K):
                        last = pe.matmul(p_o[:, u, D:], atT[:, u, k * P:(k + 1) * P], w_p[:, k], start=k == 0, stop=k == K - 1)
                    last.then_inc(o_ready, 1)


BN_EPS = 1e-3


def load_ffn1(nc, io, st):
    with nc.Block() as block:
        @block.sync
        def _(sp):
            for e in range(NE):
                for w, name in ((st.f1, "L1_ffn_W1"), (st.f2, "L1_ffn_W2"), (st.f3, "L1_ffn_Wo")):
                    sp.dma_start(w[:, e], io[name][e].rearrange("(k p) o -> p k o", p=P)).then_inc(st.ffn_w_in, 16)


def ffn1(nc, io, st):
    with ExitStack() as ctx:
        sb, ps, sem = tensors(nc, ctx)
        par = {n: sb("par_" + n, [P, NE * K]) for n in ("b1", "g1", "be1", "m1", "v1", "b2", "g2", "be2", "m2", "v2")}
        bo = sb("bo_f", [NE, D])
        cws = sb("cws_f", [P, BT * NE])
        cwT = sb("cwT_f", [NE, BT * P])
        h1 = sb("h1_f", [P, 2, K, BT * P])
        h2 = sb("h2_f", [P, 2, K, BT * P])
        p_1 = ps("p_1f", [P, K, 512])
        p_2 = ps("p_2f", [P, K, 512])
        p_y = ps("p_yf", [P, 2, BT, D])
        b_in = sem("b_in_f")
        dv = sem("dv_ffn")
        eps_added = sem("eps_added")
        roots = sem("roots")
        folded = sem("folded")
        cws_ready = sem("cws_ready_f")
        cwT_turned = sem("cwT_turned_f")
        cwT_ready = sem("cwT_ready_f")
        bias_ready = sem("bias_ready_f")
        bias_added = sem("bias_added_f")
        p1_ready = sem("p1_ready")
        h1_ready = sem("h1_ready")
        p2_ready = sem("p2_ready")
        h2_ready = sem("h2_ready")
        y_ready = sem("y_ready_f")
        y_used = sem("y_used_f")
        block = ctx.enter_context(nc.Block())

        @block.sync
        def _(sp):
            for n, t in par.items():
                sp.dma_start(t[:, :], io["ffn_" + n]).then_inc(b_in, 16)
            sp.dma_start(bo[:, :], io["L1_ffn_bo"]).then_inc(b_in, 16)
            sp.wait_ge(b_in, 16 * 11)

        @block.vector
        def _(dve):
            link = Link(dve, dv)
            dve.wait_ge(b_in, 16 * 11)
            for n in "12":
                link(dve.tensor_scalar(par["v" + n][:, :], par["v" + n][:, :], BN_EPS, None, ALU.add))
            dve.sem_inc(eps_added, 1)
            dve.wait_ge(roots, 2)
            for n in "12":
                v, g, b, m, be = (par[s + n][:, :] for s in ("v", "g", "b", "m", "be"))
                link(dve.reciprocal(v, v))
                link(dve.tensor_tensor(g, g, v, ALU.mult))
                link(dve.tensor_tensor(b, b, m, ALU.subtract))
                link(dve.tensor_tensor(b, b, g, ALU.mult))
                link(dve.tensor_tensor(b, b, be, ALU.add))
            dve.sem_inc(folded, 1)
            dve.sem_inc(y_used, 2)
            with dve.Fori(0, NBLK) as i:
                dve.wait_ge(bias_ready, i + 1)
                dve.wait_ge(y_used, NE * i + 2)
                out = st.x[:, ds(i * BT * D, BT * D)]
                dve.tensor_tensor(out, out, p_2[:, :, :].rearrange("p s n -> p (s n)"), ALU.add).then_inc(bias_added, 1)
                dve.wait_ge(bias_added, i + 1)
                for e in range(NE):
                    dve.wait_ge(y_ready, NE * i + e + 3)
                    dve.wait_ge(y_used, NE * i + e + 2)
                    for j in range(BT):
                        out = st.x[:, ds((i * BT + j) * D, D)]
                        last = dve.scalar_tensor_tensor(out=out, in0=p_y[:, e % 2, j], scalar=st.cw[:, ds((i * BT + j) * NE + e, 1)],
                                                        in1=out, op0=ALU.mult, op1=ALU.add)
                    last.then_inc(y_used, 1)

        @block.scalar
        def _(act):
            act.wait_ge(eps_added, 1)
            for n in "12":
                nc.scalar.activation(par["v" + n][:, :], par["v" + n][:, :], ACT.Sqrt).then_inc(roots, 1)
            act.wait_ge(folded, 1)
            with act.Fori(0, NBLK) as i:
                nc.scalar.copy(cws[:, :], st.cw[:, ds(i * BT * NE, BT * NE)]).then_inc(cws_ready, 1)
                act.wait_ge(cwT_turned, i + 1)
                nc.scalar.copy(cwT[:, :], p_1[0:NE, 0]).then_inc(cwT_ready, 1)

                def relu1(e):
                    for s in range(K):
                        c = e * K + s
                        act.wait_ge(p1_ready, K * (NE * i + e) + s + 1)
                        nc.scalar.activation(h1[:, e % 2, s], p_1[:, s], ACT.Relu, bias=par["b1"][:, c:c + 1],
                                             scale=par["g1"][:, c:c + 1]).then_inc(h1_ready, 1)

                def relu2(e):
                    act.wait_ge(y_ready, NE * i + e + 1)
                    for s in range(K):
                        c = e * K + s
                        act.wait_ge(p2_ready, K * (NE * i + e) + s + 1)
                        nc.scalar.activation(h2[:, e % 2, s], p_2[:, s], ACT.Relu, bias=par["b2"][:, c:c + 1],
                                             scale=par["g2"][:, c:c + 1]).then_inc(h2_ready, 1)

                relu1(0)
                for e in range(NE):
                    if e + 1 < NE:
                        relu1(e + 1)
                    relu2(e)

        @block.tensor
        def _(pe):
            pe.wait_ge(b_in, 16 * 11)
            pe.wait_ge(st.ffn_w_in, 16 * 3 * NE)
            pe.sem_inc(y_ready, 2)
            with pe.Fori(0, NBLK) as i:
                pe.wait_ge(cws_ready, i + 1)
                for j in range(BT):
                    last = pe.transpose(p_1[0:NE, 0, j * P:(j + 1) * P], cws[:, j * NE:(j + 1) * NE], st.ident[:, :])
                last.then_inc(cwT_turned, 1)
                pe.wait_ge(cwT_ready, i + 1)
                for j in range(BT):
                    last = pe.matmul(p_2[:, j // 2, (j % 2) * D:(j % 2 + 1) * D], cwT[:, j * P:(j + 1) * P], bo[:, :],
                                     start=True, stop=True)
                last.then_inc(bias_ready, 1)

                def first(e):
                    for s in range(K):
                        if e:
                            pe.wait_ge(h1_ready, K * (NE * i + e - 1) + s + 1)
                        for k in range(K):
                            last = pe.matmul(p_1[:, s], st.f1[:, e, k, s * P:(s + 1) * P], st.xnT[:, k, ds(i * BT * P, BT * P)],
                                             start=k == 0, stop=k == K - 1)
                        last.then_inc(p1_ready, 1)

                def second(e):
                    pe.wait_ge(h1_ready, K * (NE * i + e + 1))
                    for s in range(K):
                        if e:
                            pe.wait_ge(h2_ready, K * (NE * i + e - 1) + s + 1)
                        elif s == 0:
                            pe.wait_ge(bias_added, i + 1)
                        for k in range(K):
                            last = pe.matmul(p_2[:, s], st.f2[:, e, k, s * P:(s + 1) * P], h1[:, e % 2, k],
                                             start=k == 0, stop=k == K - 1)
                        last.then_inc(p2_ready, 1)

                def third(e):
                    pe.wait_ge(h2_ready, K * (NE * i + e + 1))
                    pe.wait_ge(y_used, NE * i + e + 1)
                    for j in range(BT):
                        for s in range(K):
                            last = pe.matmul(p_y[:, e % 2, j], h2[:, e % 2, s, j * P:(j + 1) * P], st.f3[:, e, s],
                                             start=s == 0, stop=s == K - 1)
                    last.then_inc(y_ready, 1)

                first(0)
                for e in range(NE):
                    second(e)
                    if e + 1 < NE:
                        first(e + 1)
                    third(e)


def finish(nc, io, st):
    with ExitStack() as ctx:
        _, _, sem = tensors(nc, ctx)
        x_out = sem("x_out")
        block = ctx.enter_context(nc.Block())

        @block.sync
        def _(sp):
            sp.dma_start(io["out"][0:(T - 1) * P, :].rearrange("(t p) d -> p t d", p=P),
                         st.x[:, 0:(T - 1) * D].rearrange("p (t d) -> p t d", d=D)).then_inc(x_out, 16)
            sp.dma_start(io["out"][(T - 1) * P:N, :], st.x[0:LAST, (T - 1) * D:T * D]).then_inc(x_out, 16)
            sp.wait_ge(x_out, 32)


def program(nc, io):
    with ExitStack() as ctx:
        st = Store()

        def sb(name, shape, dt=F32):
            return ctx.enter_context(nc.sbuf_tensor(name, shape, dt))

        st.x = sb("x", [P, T * D])
        st.ident = sb("ident", [P, P])
        st.iota = sb("iota", [P, P])
        st.rowmask = sb("rowmask", [P, 1])
        st.row_rel = sb("row_rel", [P, NSLOT], I32)
        st.row_src = sb("row_src", [P, NSLOT + 2 * SUP], I32)
        st.dloc = sb("dloc", [P, NSLOT + 2 * SUP])
        st.tile_of = sb("tile_of", [1, NSUP + 2], I32)
        st.h_table = nc.dram_tensor("h_table", (NP, R * D), F32).ap()
        st.h_rows = st.h_table.rearrange("n (r d) -> (n r) d", r=R)
        with ExitStack() as layer0:
            st.qk = layer0.enter_context(nc.sbuf_tensor("qk", [P, 2 * H * T * DH], F32))[:, :]
            st.v1 = layer0.enter_context(nc.sbuf_tensor("v1", [P, H * T * (DH + 1)], F32))[:, :]
            st.nrm = layer0.enter_context(nc.sbuf_tensor("nrm", [P, 2 * H * T], F32))
            with ExitStack() as edges:
                st.slot_hi = edges.enter_context(nc.sbuf_tensor("slot_hi", [EP, EC], F32))
                st.slot_lo = edges.enter_context(nc.sbuf_tensor("slot_lo", [EP, EC], F32))
                st.rec_hi = edges.enter_context(nc.sbuf_tensor("rec_hi", [EP, EC], F32))
                st.rec_lo = edges.enter_context(nc.sbuf_tensor("rec_lo", [EP, EC], F32))
                st.iota_s = edges.enter_context(nc.sbuf_tensor("iota_s", [P, NSLOT], F16))
                st.iota_h = edges.enter_context(nc.sbuf_tensor("iota_h", [P, P], F16))
                slot_edges(nc, io, st)
                front0(nc, io, st)
            st.mix = layer0.enter_context(nc.sbuf_tensor("mix", [P, T * D], F32))
            mix0_and_gather(nc, io, st)
            out0(nc, io, st)
        st.moe_w_in = ctx.enter_context(nc.semaphore("moe_w_in"))
        st.cw = sb("cw", [P, T * NE])
        st.xnT = sb("xnT", [P, K, NP])
        with ExitStack() as moe:
            st.w1 = moe.enter_context(nc.sbuf_tensor("w1", [P, NE, K, HID0], F32))
            st.w2 = moe.enter_context(nc.sbuf_tensor("w2", [P, NE, HS, D], F32))
            load_moe0(nc, io, st)
            normalise_and_route(nc, io, st, "L0_ffn_gate_w", "L0_ffn_gate_b", True, "_m")
            moe0(nc, io, st)
        st.g_table = nc.dram_tensor("g_table", (NP, ROW1), F32).ap()
        st.z_table = nc.dram_tensor("z_table", (NP, H), F32).ap()
        with ExitStack() as gat:
            st.s_all = gat.enter_context(nc.sbuf_tensor("s_all", [P, T * 2 * H], F32))
            st.s_max = gat.enter_context(nc.sbuf_tensor("s_max", [P, H], F32))
            st.s_unit = gat.enter_context(nc.sbuf_tensor("s_unit", [P, H], F32))
            st.wide_flag = gat.enter_context(nc.sbuf_tensor("wide_flag", [P, 1], I32))
            st.cb = gat.enter_context(nc.sbuf_tensor("cb", [P, 2, P + 4], F32))
            st.qT = gat.enter_context(nc.sbuf_tensor("qT", [P, T * D], F32))
            st.acc = gat.enter_context(nc.sbuf_tensor("acc", [P, T * ROW1], F32))
            front1(nc, io, st)
            segment_bound(nc, io, st)
            attend(nc, io, st)
            out1(nc, io, st)
        st.ffn_w_in = ctx.enter_context(nc.semaphore("ffn_w_in"))
        st.f1 = sb("f1", [P, NE, K, D])
        st.f2 = sb("f2", [P, NE, K, D])
        st.f3 = sb("f3", [P, NE, K, D])
        load_ffn1(nc, io, st)
        normalise_and_route(nc, io, st, "L1_ffn_Wr", "L1_ffn_br", False, "_f")
        ffn1(nc, io, st)
        finish(nc, io, st)


def kernel(**inputs):
    import numpy as _np
    import concourse.bacc as _bacc
    from concourse import mybir as _mybir
    from concourse.bass_utils import run_bass_kernel_spmd as _run

    arrays = {name: _np.asarray(a) for name, a in inputs.items()}
    arrays["wqkv0"] = arrays.pop("L0_mix_Wqkv").T
    arrays["wproj0"] = arrays.pop("L0_mix_Wproj").T
    arrays["temp0"] = arrays.pop("L0_mix_temperature").reshape(-1)
    arrays["moe_b1"] = arrays.pop("L0_ffn_b1").reshape(8, 4, 128).transpose(2, 0, 1).reshape(128, 32)
    arrays["gat_w"] = arrays.pop("L1_gnn_W").transpose(1, 0, 2).reshape(256, 512)
    arrays["wq1"] = arrays.pop("L1_mix_Wq").T
    arrays["wkv1"] = arrays.pop("L1_mix_Wkv").T
    arrays["wproj1"] = arrays.pop("L1_mix_Wproj").T
    for name in ("b1", "g1", "be1", "m1", "v1", "b2", "g2", "be2", "m2", "v2"):
        arrays["ffn_" + name] = arrays.pop("L1_ffn_" + name).reshape(8, 2, 128).transpose(2, 0, 1).reshape(128, 16)
    nc = _bacc.Bacc("TRN2", target_bir_lowering=False, num_devices=1)
    io, fed = {}, {}
    for name, a in arrays.items():
        a = _np.ascontiguousarray(a)
        fed[f"in_{name}"] = a
        io[name] = nc.dram_tensor(f"in_{name}", a.shape, _mybir.dt.from_np(a.dtype), kind="ExternalInput").ap()
    io["out"] = nc.dram_tensor("out_0", (2500, 256), _mybir.dt.float32, kind="ExternalOutput").ap()
    program(nc, io)
    r = _run(nc, [fed], core_ids=[0])
    return r.results[0]["out_0"]
```
